# Optimizing a Trainium2 kernel written in Bass

```python
import numpy as np
import jax
import jax.numpy as jnp

def _softmax(x, axis=-1):
    return jax.nn.softmax(x, axis=axis)

def _gelu(x):
    return jax.nn.gelu(x, approximate=True)

def _silu(x):
    return jax.nn.silu(x)

def _sigmoid(x):
    return jax.nn.sigmoid(x)

def _layernorm(x, axis=-1, eps=1e-05):
    m = jnp.mean(x, axis=axis, keepdims=True)
    v = jnp.var(x, axis=axis, keepdims=True)
    return (x - m) / jnp.sqrt(v + eps)

def _scatter_add(tgt, idx, src, axis=0):
    return tgt.at[idx].add(src)

def _segment_sum(src, seg, n):
    return jax.ops.segment_sum(src, seg, n)
kernel_name = 'mk_decoder_postln_d4_seqx_r8_8aa329'

def setup_inputs(seed: int=0):
    np.random.seed(seed)
    _w = jnp.asarray

    def _rec_inputs():
        import jax
        import jax.numpy as jnp
        _rk = jax.random.key(seed)
        x = -0.0002928 + 1 * jax.random.normal(jax.random.fold_in(_rk, 1), (4, 512, 128), jnp.float32)
        _lenS = 512 - jax.random.randint(jax.random.fold_in(_rk, 7), (4,), 0, max(1, 512 // 4) + 1, jnp.int32)
        _lenS2 = 154 - jax.random.randint(jax.random.fold_in(_rk, 8), (4,), 0, max(1, 154 // 4) + 1, jnp.int32)
        _ctx_1024P = jax.random.normal(jax.random.fold_in(_rk, 11), (4, 16, 128), jnp.float32)
        _ctx_1024c = jax.random.dirichlet(jax.random.fold_in(_rk, 511), 0.3 * jnp.ones((16,), jnp.float32), (4, 154))
        _ctx_1024t = jnp.einsum('bsk,bkd->bsd', _ctx_1024c, _ctx_1024P)
        _ctx_1024t = _ctx_1024t * jax.lax.rsqrt(jnp.mean(jnp.square(_ctx_1024t)) + 1e-12) * 0.953939
        ctx_1024 = -1.39393e-06 + 0.999914 * (_ctx_1024t + 0.3 * jax.random.normal(jax.random.fold_in(_rk, 611), (4, 154, 128), jnp.float32))
        _validS = jnp.arange(512)[None, :] < _lenS[:, None]
        _validS2 = jnp.arange(154)[None, :] < _lenS2[:, None]
        _causal = jnp.tril(jnp.ones((512, 512), dtype=bool))
        mask_BxS2_bf1 = jnp.ones((4, 154), dtype=bool)
        mask_1x1xSxS2_bk0 = jnp.logical_not(jnp.broadcast_to(_validS2[0:1, None, None, :], (1, 1, 512, 154)))
        return (x, ctx_1024, mask_BxS2_bf1, mask_1x1xSxS2_bk0)
    x, ctx_1024, mask_BxS2_bf1, mask_1x1xSxS2_bk0 = _rec_inputs()

    def _L0_attn_setup():
        import jax, jax.numpy as jnp
        import numpy as np
        import math
        NUM_HEADS = 16
        DIM = 128
        DH = DIM // NUM_HEADS
        THETA = 10000.0
        SCALE_BASE = 512.0

        def _rotate_half(x):
            x = x.reshape(*x.shape[:-1], -1, 2)
            x1, x2 = (x[..., 0], x[..., 1])
            return jnp.stack((-x2, x1), axis=-1).reshape(*x1.shape[:-1], -1)

        def _xpos_rotate(q, k):
            s = q.shape[2]
            t = jnp.arange(s, dtype=jnp.float32)
            inv_freq = 1.0 / THETA ** (jnp.arange(0, DH, 2, dtype=jnp.float32) / DH)
            freqs = t[:, None] * inv_freq[None, :]
            freqs = jnp.repeat(freqs, 2, axis=-1)
            cos, sin = (jnp.cos(freqs), jnp.sin(freqs))
            base = (jnp.arange(0, DH, 2, dtype=jnp.float32) + 0.4 * DH) / (1.4 * DH)
            power = (t - s // 2) / SCALE_BASE
            scale = base[None, :] ** power[:, None]
            scale = jnp.concatenate((scale, scale), axis=-1)
            q = q * cos * scale + _rotate_half(q) * sin * scale
            inv_scale = 1.0 / scale
            k = k * cos * inv_scale + _rotate_half(k) * sin * inv_scale
            return (q, k)
        key = jax.random.key(seed)
        ks = jax.random.split(key, 5)
        b, s = (2, 256)
        w_scale = DIM ** (-0.5)
        return {'x': jax.random.normal(ks[0], (b, s, DIM), jnp.float32), 'Wq': jax.random.normal(ks[1], (DIM, DIM), jnp.float32) * w_scale, 'bq': jnp.zeros((DIM,), jnp.float32), 'Wk': jax.random.normal(ks[2], (DIM, DIM), jnp.float32) * w_scale, 'bk': jnp.zeros((DIM,), jnp.float32), 'Wv': jax.random.normal(ks[3], (DIM, DIM), jnp.float32) * w_scale, 'bv': jnp.zeros((DIM,), jnp.float32), 'Wo': jax.random.normal(ks[4], (DIM, DIM), jnp.float32) * w_scale, 'bo': jnp.zeros((DIM,), jnp.float32)}
    _L0_attn_all = _L0_attn_setup()
    _L0_attn_in = {k: v for k, v in _L0_attn_all.items() if k in ('Wq', 'bq', 'Wk', 'bk', 'Wv', 'bv', 'Wo', 'bo')}
    del _L0_attn_all

    def _L0_xattn_setup():
        import jax, jax.numpy as jnp
        import numpy as np
        D_MODEL = 128
        N_HEAD = 16

        def _split_heads(x, n_head):
            b, s, d = x.shape
            return x.reshape(b, s, n_head, d // n_head).transpose(0, 2, 1, 3)
        key = jax.random.key(seed)
        ks = jax.random.split(key, 11)
        B, S, D = (2, 256, D_MODEL)
        scale = 1.0 / np.sqrt(D)
        inp = {'query_tensor': jax.random.normal(ks[0], (B, S, D), jnp.float32), 'key_tensor': jax.random.normal(ks[1], (B, S, D), jnp.float32), 'value_tensor': jax.random.normal(ks[2], (B, S, D), jnp.float32), 'w_q': jax.random.normal(ks[3], (D, D), jnp.float32) * scale, 'b_q': jnp.zeros((D,), jnp.float32), 'w_k': jax.random.normal(ks[4], (D, D), jnp.float32) * scale, 'b_k': jnp.zeros((D,), jnp.float32), 'w_v': jax.random.normal(ks[5], (D, D), jnp.float32) * scale, 'b_v': jnp.zeros((D,), jnp.float32), 'w_out': jax.random.normal(ks[6], (D, D), jnp.float32) * scale, 'b_out': jnp.zeros((D,), jnp.float32)}
        return inp
    _L0_xattn_all = _L0_xattn_setup()
    _L0_xattn_in = {k: v for k, v in _L0_xattn_all.items() if k in ('w_q', 'b_q', 'w_k', 'b_k', 'w_v', 'b_v', 'w_out', 'b_out')}
    del _L0_xattn_all

    def _L0_ffn_setup():
        import jax, jax.numpy as jnp
        import numpy as np
        B, S, D_MODEL, D_HIDDEN = (4, 256, 128, 512)

        def act_quant(x):
            scale = 127.0 / jnp.clip(jnp.max(jnp.abs(x), axis=-1, keepdims=True), 1e-05)
            return jnp.clip(jnp.round(x * scale), -128, 127) / scale

        def weight_quant(w):
            scale = 1.0 / jnp.clip(jnp.mean(jnp.abs(w)), 1e-05)
            return jnp.clip(jnp.round(w * scale), -1, 1) / scale

        def bit_linear(x, w):
            xq = x + jax.lax.stop_gradient(act_quant(x) - x)
            wq = w + jax.lax.stop_gradient(weight_quant(w) - w)
            return jnp.einsum('bsd,hd->bsh', xq, wq)

        def depthwise_conv1d(x_bcl, w, b):
            y = jax.lax.conv_general_dilated(x_bcl, w, window_strides=(1,), padding=[(1, 1)], dimension_numbers=('NCH', 'OIH', 'NCH'), feature_group_count=x_bcl.shape[1])
            return y + b[None, :, None]
        key = jax.random.key(seed)
        ks = jax.random.split(key, 5)
        lim1 = 1.0 / np.sqrt(D_MODEL)
        lim2 = 1.0 / np.sqrt(D_HIDDEN)
        limc = 1.0 / np.sqrt(3.0)
        return {'x': jax.random.normal(ks[0], (B, S, D_MODEL), dtype=jnp.float32), 'w1': jax.random.uniform(ks[1], (D_HIDDEN, D_MODEL), jnp.float32, -lim1, lim1), 'conv_w': jax.random.uniform(ks[2], (D_HIDDEN, 1, 3), jnp.float32, -limc, limc), 'conv_b': jax.random.uniform(ks[3], (D_HIDDEN,), jnp.float32, -limc, limc), 'w2': jax.random.uniform(ks[4], (D_MODEL, D_HIDDEN), jnp.float32, -lim2, lim2)}
    _L0_ffn_all = _L0_ffn_setup()
    _L0_ffn_in = {k: v for k, v in _L0_ffn_all.items() if k in ('w1', 'conv_w', 'conv_b', 'w2')}
    del _L0_ffn_all

    def _L1_attn_setup():
        import jax, jax.numpy as jnp
        import numpy as np
        N_HEADS = 16
        SCALE = 8.0
        key = jax.random.key(seed)
        k1, k2, k3, k4 = jax.random.split(key, 4)
        b, n, d_model, inner = (8, 256, 128, 128)
        x = jax.random.normal(k1, (b, n, d_model), dtype=jnp.float32)
        Wqkv = jax.random.normal(k2, (3 * inner, d_model), dtype=jnp.float32) * (1.0 / np.sqrt(d_model))
        Wproj = jax.random.normal(k3, (d_model, inner), dtype=jnp.float32) * (1.0 / np.sqrt(inner))
        bproj = jax.random.normal(k4, (d_model,), dtype=jnp.float32) * 0.01
        return {'x': x, 'Wqkv': Wqkv, 'Wproj': Wproj, 'bproj': bproj}
    _L1_attn_all = _L1_attn_setup()
    _L1_attn_in = {k: v for k, v in _L1_attn_all.items() if k in ('Wqkv', 'Wproj', 'bproj')}
    del _L1_attn_all

    def _L1_xattn_setup():
        import jax, jax.numpy as jnp
        import numpy as np
        N_HEADS = 16
        D_MODEL = 128
        HEAD_DIM = D_MODEL // N_HEADS
        MASK_FILL = -100000000.0

        def _split_heads(x):
            B, S, _ = x.shape
            return x.reshape(B, S, N_HEADS, HEAD_DIM).transpose(0, 2, 1, 3)
        key = jax.random.key(seed)
        ks = jax.random.split(key, 12)
        B, L, P = (2, 256, 256)
        s = 1.0 / np.sqrt(D_MODEL).astype(np.float32)
        inp = {'q': jax.random.normal(ks[0], (B, L, D_MODEL), dtype=jnp.float32), 'k': jax.random.normal(ks[1], (B, P, D_MODEL), dtype=jnp.float32), 'v': jax.random.normal(ks[2], (B, P, D_MODEL), dtype=jnp.float32), 'attention_mask': jnp.ones((B, P), dtype=bool), 'Wq': jax.random.normal(ks[3], (D_MODEL, D_MODEL), dtype=jnp.float32) * s, 'bq': jnp.zeros((D_MODEL,), dtype=jnp.float32), 'Wk': jax.random.normal(ks[4], (D_MODEL, D_MODEL), dtype=jnp.float32) * s, 'bk': jnp.zeros((D_MODEL,), dtype=jnp.float32), 'Wv': jax.random.normal(ks[5], (D_MODEL, D_MODEL), dtype=jnp.float32) * s, 'bv': jnp.zeros((D_MODEL,), dtype=jnp.float32), 'Wo': jax.random.normal(ks[6], (D_MODEL, D_MODEL), dtype=jnp.float32) * s, 'bo': jnp.zeros((D_MODEL,), dtype=jnp.float32)}
        return inp
    _L1_xattn_all = _L1_xattn_setup()
    _L1_xattn_in = {k: v for k, v in _L1_xattn_all.items() if k in ('Wq', 'bq', 'Wk', 'bk', 'Wv', 'bv', 'Wo', 'bo')}
    del _L1_xattn_all

    def _L1_ffn_setup():
        import math
        import jax, jax.numpy as jnp
        from jax import lax
        import numpy as np
        E = 16
        K = 2
        CF = 1.25
        key = jax.random.key(seed)
        k0, k1, k2, k3, k4 = jax.random.split(key, 5)
        B, S, D, H = (2, 256, 128, 128)
        scale = 0.02
        return {'x': jax.random.normal(k0, (B, S, D), dtype=jnp.float32), 'router_w': jax.random.normal(k1, (D, E), dtype=jnp.float32) * scale, 'gate_w': jax.random.normal(k2, (E, D, H), dtype=jnp.float32) * scale, 'up_w': jax.random.normal(k3, (E, D, H), dtype=jnp.float32) * scale, 'down_w': jax.random.normal(k4, (E, H, D), dtype=jnp.float32) * scale}
    _L1_ffn_all = _L1_ffn_setup()
    _L1_ffn_in = {k: v for k, v in _L1_ffn_all.items() if k in ('router_w', 'gate_w', 'up_w', 'down_w')}
    del _L1_ffn_all

    def _L2_attn_setup():
        import math
        import jax, jax.numpy as jnp
        import numpy as np
        D = 128
        NH = 16
        DH = D // NH

        def _rope(q, k, base=10000.0):
            half = q.shape[-1] // 2
            freqs = jnp.arange(half, dtype=q.dtype) / half
            theta = 1.0 / base ** freqs
            t = jnp.arange(q.shape[-2], dtype=q.dtype)
            ang = t[:, None] * theta[None, :]
            cos = jnp.cos(ang)[None, None, :, :]
            sin = jnp.sin(ang)[None, None, :, :]

            def rot(x):
                x1, x2 = (x[..., :half], x[..., half:])
                return jnp.concatenate([x1 * cos - x2 * sin, x1 * sin + x2 * cos], axis=-1)
            return (rot(q), rot(k))
        key = jax.random.key(seed)
        k1, k2, k3 = jax.random.split(key, 3)
        x = jax.random.normal(k1, (2, 256, D), dtype=jnp.float32)
        s = 1.0 / math.sqrt(D)
        W_qkv = jax.random.normal(k2, (D, 3 * D), dtype=jnp.float32) * s
        W_o = jax.random.normal(k3, (D, D), dtype=jnp.float32) * s
        return {'x': x, 'W_qkv': W_qkv, 'W_o': W_o}
    _L2_attn_all = _L2_attn_setup()
    _L2_attn_in = {k: v for k, v in _L2_attn_all.items() if k in ('W_qkv', 'W_o')}
    del _L2_attn_all

    def _L2_xattn_setup():
        import jax, jax.numpy as jnp
        import numpy as np
        B, S, E, H = (2, 256, 128, 16)
        D = E // H
        key = jax.random.key(seed)
        ks = jax.random.split(key, 8)
        inp = {'key': jax.random.normal(ks[0], (B, S, E), dtype=jnp.float32), 'query': jax.random.normal(ks[1], (B, S, E), dtype=jnp.float32), 'value': jax.random.normal(ks[2], (B, S, E), dtype=jnp.float32), 'mask': jnp.tril(jnp.ones((S, S), dtype=bool))[None, None, :, :], 'Wq': jax.random.normal(ks[3], (D, D), dtype=jnp.float32) / np.sqrt(D), 'Wk': jax.random.normal(ks[4], (D, D), dtype=jnp.float32) / np.sqrt(D), 'Wv': jax.random.normal(ks[5], (D, D), dtype=jnp.float32) / np.sqrt(D), 'Wo': jax.random.normal(ks[6], (E, E), dtype=jnp.float32) / np.sqrt(E), 'bo': jax.random.normal(ks[7], (E,), dtype=jnp.float32) * 0.01}
        return inp
    _L2_xattn_all = _L2_xattn_setup()
    _L2_xattn_in = {k: v for k, v in _L2_xattn_all.items() if k in ('Wq', 'Wk', 'Wv', 'Wo', 'bo')}
    del _L2_xattn_all

    def _L2_ffn_setup():
        import jax, jax.numpy as jnp
        import numpy as np
        D_IN, D_HID = (128, 512)

        def _ternary(key, shape):
            return jax.random.randint(key, shape, -1, 2).astype(jnp.float32)

        def _tlin(x, w, s):
            return jnp.einsum('bsi,oi->bso', x, w) * s
        key = jax.random.key(seed)
        ks = jax.random.split(key, 12)
        inv = lambda fan: 1.0 / np.sqrt(fan).astype(np.float32)
        return {'x': jax.random.normal(ks[0], (4, 256, D_IN), dtype=jnp.float32), 'w1_w': _ternary(ks[1], (D_HID, D_IN)), 'w1_s': jax.random.uniform(ks[2], (D_HID,), dtype=jnp.float32) * inv(D_IN), 'w2_w': _ternary(ks[3], (D_HID, D_IN)), 'w2_s': jax.random.uniform(ks[4], (D_HID,), dtype=jnp.float32) * inv(D_IN), 'h1_w': _ternary(ks[5], (D_HID, D_HID)), 'h1_s': jax.random.uniform(ks[6], (D_HID,), dtype=jnp.float32) * inv(D_HID), 'h2_w': _ternary(ks[7], (D_HID, D_HID)), 'h2_s': jax.random.uniform(ks[8], (D_HID,), dtype=jnp.float32) * inv(D_HID), 'w3_w': _ternary(ks[9], (D_IN, D_HID)), 'w3_s': jax.random.uniform(ks[10], (D_IN,), dtype=jnp.float32) * inv(D_HID)}
    _L2_ffn_all = _L2_ffn_setup()
    _L2_ffn_in = {k: v for k, v in _L2_ffn_all.items() if k in ('w1_w', 'w1_s', 'w2_w', 'w2_s', 'h1_w', 'h1_s', 'h2_w', 'h2_s', 'w3_w', 'w3_s')}
    del _L2_ffn_all

    def _L3_attn_setup():
        import jax, jax.numpy as jnp
        import numpy as np
        MAX_DISTANCE = 10
        SCALE = 0.01

        def distance_bias(seq_len):
            idx = jnp.arange(seq_len, dtype=jnp.float32)
            d = jnp.abs(idx[None, :] - idx[:, None])
            return jnp.clip(d, 0.0, MAX_DISTANCE) * SCALE
        key = jax.random.key(seed)
        k1, k2 = jax.random.split(key)
        B, S, D_IN, D_OUT = (8, 256, 128, 128)
        x = jax.random.normal(k1, (B, S, D_IN), dtype=jnp.float32)
        W = jax.random.normal(k2, (D_IN, D_OUT), dtype=jnp.float32) * (1.0 / np.sqrt(D_IN))
        b = jnp.zeros((D_OUT,), dtype=jnp.float32)
        return {'x': x, 'W': W, 'b': b}
    _L3_attn_all = _L3_attn_setup()
    _L3_attn_in = {k: v for k, v in _L3_attn_all.items() if k in ('W', 'b')}
    del _L3_attn_all

    def _L3_xattn_setup():
        import jax, jax.numpy as jnp
        import numpy as np
        EMBED_DIM = 128
        NUM_HEADS = 16
        HEAD_DIM = EMBED_DIM // NUM_HEADS
        B, L = (4, 256)
        NEG_INF = jnp.float32(-1e+30)

        def _split_heads(x):
            b, l, _ = x.shape
            return x.reshape(b, l, NUM_HEADS, HEAD_DIM).transpose(0, 2, 1, 3)
        key = jax.random.key(seed)
        ks = jax.random.split(key, 11)
        s = 1.0 / np.sqrt(EMBED_DIM)
        d = {'query': jax.random.normal(ks[0], (B, L, EMBED_DIM), jnp.float32), 'key': jax.random.normal(ks[1], (B, L, EMBED_DIM), jnp.float32), 'value': jax.random.normal(ks[2], (B, L, EMBED_DIM), jnp.float32), 'Wq': jax.random.uniform(ks[3], (EMBED_DIM, EMBED_DIM), jnp.float32, -s, s), 'bq': jax.random.uniform(ks[4], (EMBED_DIM,), jnp.float32, -s, s), 'Wk': jax.random.uniform(ks[5], (EMBED_DIM, EMBED_DIM), jnp.float32, -s, s), 'bk': jax.random.uniform(ks[6], (EMBED_DIM,), jnp.float32, -s, s), 'Wv': jax.random.uniform(ks[7], (EMBED_DIM, EMBED_DIM), jnp.float32, -s, s), 'bv': jax.random.uniform(ks[8], (EMBED_DIM,), jnp.float32, -s, s), 'Wo': jax.random.uniform(ks[9], (EMBED_DIM, EMBED_DIM), jnp.float32, -s, s), 'bo': jax.random.uniform(ks[10], (EMBED_DIM,), jnp.float32, -s, s)}
        return d
    _L3_xattn_all = _L3_xattn_setup()
    _L3_xattn_in = {k: v for k, v in _L3_xattn_all.items() if k in ('Wq', 'bq', 'Wk', 'bk', 'Wv', 'bv', 'Wo', 'bo')}
    del _L3_xattn_all

    def _L3_ffn_setup():
        import jax, jax.numpy as jnp
        import numpy as np
        import math
        GOLDEN_CENTER = 1.0 / math.e
        GOLDEN_LOWER = 0.5 - math.log(4.0 / 3.0)
        GOLDEN_UPPER = 0.5
        B, T, D = (4, 256, 128)
        E = 8
        I = 512 // (E // 2)

        def _routing_weights(x, Wr, temperature):
            inh = jax.nn.sigmoid(x @ Wr / temperature)
            in_zone = (inh >= GOLDEN_LOWER) & (inh <= GOLDEN_UPPER)
            dist = jnp.abs(inh - GOLDEN_CENTER)
            w = jnp.exp(-dist / 0.1) * in_zone.astype(x.dtype)
            wsum = w.sum(axis=-1, keepdims=True)
            no_expert = wsum < 1e-08
            fb = jnp.exp(-dist / 0.3)
            _, top2 = jax.lax.top_k(fb, 2)
            fb_mask = jax.nn.one_hot(top2, E, dtype=x.dtype).sum(axis=-2)
            fb_w = fb * fb_mask
            fb_w = fb_w / jnp.clip(fb_w.sum(axis=-1, keepdims=True), 1e-08)
            w = jnp.where(no_expert, fb_w, w)
            wsum = w.sum(axis=-1, keepdims=True)
            return w / jnp.clip(wsum, 1e-08)
        key = jax.random.key(seed)
        k = jax.random.split(key, 6)
        s_d = 1.0 / math.sqrt(D)
        s_i = 1.0 / math.sqrt(I)
        return {'x': jax.random.normal(k[0], (B, T, D), jnp.float32), 'Wg': jax.random.normal(k[1], (E, D, I), jnp.float32) * s_d, 'Wu': jax.random.normal(k[2], (E, D, I), jnp.float32) * s_d, 'Wd': jax.random.normal(k[3], (E, I, D), jnp.float32) * s_i, 'Wr': jax.random.normal(k[4], (D, E), jnp.float32) * s_d, 'temperature': jnp.ones((1,), jnp.float32)}
    _L3_ffn_all = _L3_ffn_setup()
    _L3_ffn_in = {k: v for k, v in _L3_ffn_all.items() if k in ('Wg', 'Wu', 'Wd', 'Wr', 'temperature')}
    del _L3_ffn_all
    return {'x': x, 'ctx_1024': ctx_1024, 'mask_BxS2_bf1': mask_BxS2_bf1, 'mask_1x1xSxS2_bk0': mask_1x1xSxS2_bk0, 'L0_attn_Wq': _L0_attn_in['Wq'], 'L0_attn_bq': _L0_attn_in['bq'], 'L0_attn_Wk': _L0_attn_in['Wk'], 'L0_attn_bk': _L0_attn_in['bk'], 'L0_attn_Wv': _L0_attn_in['Wv'], 'L0_attn_bv': _L0_attn_in['bv'], 'L0_attn_Wo': _L0_attn_in['Wo'], 'L0_attn_bo': _L0_attn_in['bo'], 'L0_xattn_w_q': _L0_xattn_in['w_q'], 'L0_xattn_b_q': _L0_xattn_in['b_q'], 'L0_xattn_w_k': _L0_xattn_in['w_k'], 'L0_xattn_b_k': _L0_xattn_in['b_k'], 'L0_xattn_w_v': _L0_xattn_in['w_v'], 'L0_xattn_b_v': _L0_xattn_in['b_v'], 'L0_xattn_w_out': _L0_xattn_in['w_out'], 'L0_xattn_b_out': _L0_xattn_in['b_out'], 'L0_ffn_w1': _L0_ffn_in['w1'], 'L0_ffn_conv_w': _L0_ffn_in['conv_w'], 'L0_ffn_conv_b': _L0_ffn_in['conv_b'], 'L0_ffn_w2': _L0_ffn_in['w2'], 'L1_attn_Wqkv': _L1_attn_in['Wqkv'], 'L1_attn_Wproj': _L1_attn_in['Wproj'], 'L1_attn_bproj': _L1_attn_in['bproj'], 'L1_xattn_Wq': _L1_xattn_in['Wq'], 'L1_xattn_bq': _L1_xattn_in['bq'], 'L1_xattn_Wk': _L1_xattn_in['Wk'], 'L1_xattn_bk': _L1_xattn_in['bk'], 'L1_xattn_Wv': _L1_xattn_in['Wv'], 'L1_xattn_bv': _L1_xattn_in['bv'], 'L1_xattn_Wo': _L1_xattn_in['Wo'], 'L1_xattn_bo': _L1_xattn_in['bo'], 'L1_ffn_router_w': _L1_ffn_in['router_w'], 'L1_ffn_gate_w': _L1_ffn_in['gate_w'], 'L1_ffn_up_w': _L1_ffn_in['up_w'], 'L1_ffn_down_w': _L1_ffn_in['down_w'], 'L2_attn_W_qkv': _L2_attn_in['W_qkv'], 'L2_attn_W_o': _L2_attn_in['W_o'], 'L2_xattn_Wq': _L2_xattn_in['Wq'], 'L2_xattn_Wk': _L2_xattn_in['Wk'], 'L2_xattn_Wv': _L2_xattn_in['Wv'], 'L2_xattn_Wo': _L2_xattn_in['Wo'], 'L2_xattn_bo': _L2_xattn_in['bo'], 'L2_ffn_w1_w': _L2_ffn_in['w1_w'], 'L2_ffn_w1_s': _L2_ffn_in['w1_s'], 'L2_ffn_w2_w': _L2_ffn_in['w2_w'], 'L2_ffn_w2_s': _L2_ffn_in['w2_s'], 'L2_ffn_h1_w': _L2_ffn_in['h1_w'], 'L2_ffn_h1_s': _L2_ffn_in['h1_s'], 'L2_ffn_h2_w': _L2_ffn_in['h2_w'], 'L2_ffn_h2_s': _L2_ffn_in['h2_s'], 'L2_ffn_w3_w': _L2_ffn_in['w3_w'], 'L2_ffn_w3_s': _L2_ffn_in['w3_s'], 'L3_attn_W': _L3_attn_in['W'], 'L3_attn_b': _L3_attn_in['b'], 'L3_xattn_Wq': _L3_xattn_in['Wq'], 'L3_xattn_bq': _L3_xattn_in['bq'], 'L3_xattn_Wk': _L3_xattn_in['Wk'], 'L3_xattn_bk': _L3_xattn_in['bk'], 'L3_xattn_Wv': _L3_xattn_in['Wv'], 'L3_xattn_bv': _L3_xattn_in['bv'], 'L3_xattn_Wo': _L3_xattn_in['Wo'], 'L3_xattn_bo': _L3_xattn_in['bo'], 'L3_ffn_Wg': _L3_ffn_in['Wg'], 'L3_ffn_Wu': _L3_ffn_in['Wu'], 'L3_ffn_Wd': _L3_ffn_in['Wd'], 'L3_ffn_Wr': _L3_ffn_in['Wr'], 'L3_ffn_temperature': _L3_ffn_in['temperature']}

def reference(x, ctx_1024, mask_BxS2_bf1, mask_1x1xSxS2_bk0, L0_attn_Wq, L0_attn_bq, L0_attn_Wk, L0_attn_bk, L0_attn_Wv, L0_attn_bv, L0_attn_Wo, L0_attn_bo, L0_xattn_w_q, L0_xattn_b_q, L0_xattn_w_k, L0_xattn_b_k, L0_xattn_w_v, L0_xattn_b_v, L0_xattn_w_out, L0_xattn_b_out, L0_ffn_w1, L0_ffn_conv_w, L0_ffn_conv_b, L0_ffn_w2, L1_attn_Wqkv, L1_attn_Wproj, L1_attn_bproj, L1_xattn_Wq, L1_xattn_bq, L1_xattn_Wk, L1_xattn_bk, L1_xattn_Wv, L1_xattn_bv, L1_xattn_Wo, L1_xattn_bo, L1_ffn_router_w, L1_ffn_gate_w, L1_ffn_up_w, L1_ffn_down_w, L2_attn_W_qkv, L2_attn_W_o, L2_xattn_Wq, L2_xattn_Wk, L2_xattn_Wv, L2_xattn_Wo, L2_xattn_bo, L2_ffn_w1_w, L2_ffn_w1_s, L2_ffn_w2_w, L2_ffn_w2_s, L2_ffn_h1_w, L2_ffn_h1_s, L2_ffn_h2_w, L2_ffn_h2_s, L2_ffn_w3_w, L2_ffn_w3_s, L3_attn_W, L3_attn_b, L3_xattn_Wq, L3_xattn_bq, L3_xattn_Wk, L3_xattn_bk, L3_xattn_Wv, L3_xattn_bv, L3_xattn_Wo, L3_xattn_bo, L3_ffn_Wg, L3_ffn_Wu, L3_ffn_Wd, L3_ffn_Wr, L3_ffn_temperature):
    import jax
    import jax.numpy as jnp

    def _L0_attn_ref(x, Wq, bq, Wk, bk, Wv, bv, Wo, bo):
        import jax, jax.numpy as jnp
        import numpy as np
        import math
        NUM_HEADS = 16
        DIM = 128
        DH = DIM // NUM_HEADS
        THETA = 10000.0
        SCALE_BASE = 512.0

        def _rotate_half(x):
            x = x.reshape(*x.shape[:-1], -1, 2)
            x1, x2 = (x[..., 0], x[..., 1])
            return jnp.stack((-x2, x1), axis=-1).reshape(*x1.shape[:-1], -1)

        def _xpos_rotate(q, k):
            s = q.shape[2]
            t = jnp.arange(s, dtype=jnp.float32)
            inv_freq = 1.0 / THETA ** (jnp.arange(0, DH, 2, dtype=jnp.float32) / DH)
            freqs = t[:, None] * inv_freq[None, :]
            freqs = jnp.repeat(freqs, 2, axis=-1)
            cos, sin = (jnp.cos(freqs), jnp.sin(freqs))
            base = (jnp.arange(0, DH, 2, dtype=jnp.float32) + 0.4 * DH) / (1.4 * DH)
            power = (t - s // 2) / SCALE_BASE
            scale = base[None, :] ** power[:, None]
            scale = jnp.concatenate((scale, scale), axis=-1)
            q = q * cos * scale + _rotate_half(q) * sin * scale
            inv_scale = 1.0 / scale
            k = k * cos * inv_scale + _rotate_half(k) * sin * inv_scale
            return (q, k)
        b, s, _ = x.shape

        def split_heads(t):
            return t.reshape(b, s, NUM_HEADS, DH).transpose(0, 2, 1, 3)
        q_mat = split_heads(x @ Wq.T + bq)
        k_mat = split_heads(x @ Wv.T + bv)
        v_mat = split_heads(x @ Wk.T + bk)
        q_mat, k_mat = _xpos_rotate(q_mat, k_mat)
        scores = jnp.einsum('bhqd,bhkd->bhqk', q_mat, k_mat) / math.sqrt(DH * NUM_HEADS)
        causal = jnp.tril(jnp.ones((s, s), dtype=bool))
        scores = jnp.where(causal[None, None], scores, -jnp.inf)
        weights = jax.nn.softmax(scores, axis=-1)
        inter = jnp.einsum('bhqk,bhkd->bhqd', weights, v_mat)
        inter = inter.transpose(0, 2, 1, 3).reshape(b, s, DIM)
        return inter @ Wo.T + bo

    def _L0_xattn_ref(query_tensor, key_tensor, value_tensor, w_q, b_q, w_k, b_k, w_v, b_v, w_out, b_out):
        import jax, jax.numpy as jnp
        import numpy as np
        D_MODEL = 128
        N_HEAD = 16

        def _split_heads(x, n_head):
            b, s, d = x.shape
            return x.reshape(b, s, n_head, d // n_head).transpose(0, 2, 1, 3)
        q = query_tensor @ w_q.T + b_q
        k = key_tensor @ w_k.T + b_k
        v = value_tensor @ w_v.T + b_v
        q = _split_heads(q, N_HEAD)
        k = _split_heads(k, N_HEAD)
        v = _split_heads(v, N_HEAD)
        d_k = k.shape[-1]
        scores = jnp.einsum('bhqd,bhkd->bhqk', q, k) / jnp.sqrt(jnp.float32(d_k))
        attn = jax.nn.softmax(scores, axis=-1)
        ctx = jnp.einsum('bhqk,bhkd->bhqd', attn, v)
        b, h, s, dk = ctx.shape
        ctx = ctx.transpose(0, 2, 1, 3).reshape(b, s, h * dk)
        return ctx @ w_out.T + b_out

    def _L0_ffn_ref(x, w1, conv_w, conv_b, w2):
        import jax, jax.numpy as jnp
        import numpy as np
        B, S, D_MODEL, D_HIDDEN = (4, 256, 128, 512)

        def act_quant(x):
            scale = 127.0 / jnp.clip(jnp.max(jnp.abs(x), axis=-1, keepdims=True), 1e-05)
            return jnp.clip(jnp.round(x * scale), -128, 127) / scale

        def weight_quant(w):
            scale = 1.0 / jnp.clip(jnp.mean(jnp.abs(w)), 1e-05)
            return jnp.clip(jnp.round(w * scale), -1, 1) / scale

        def bit_linear(x, w):
            xq = x + jax.lax.stop_gradient(act_quant(x) - x)
            wq = w + jax.lax.stop_gradient(weight_quant(w) - w)
            return jnp.einsum('bsd,hd->bsh', xq, wq)

        def depthwise_conv1d(x_bcl, w, b):
            y = jax.lax.conv_general_dilated(x_bcl, w, window_strides=(1,), padding=[(1, 1)], dimension_numbers=('NCH', 'OIH', 'NCH'), feature_group_count=x_bcl.shape[1])
            return y + b[None, :, None]
        h = bit_linear(x, w1)
        h = depthwise_conv1d(h.transpose(0, 2, 1), conv_w, conv_b)
        h = h.transpose(0, 2, 1)
        h = jax.nn.silu(h)
        return bit_linear(h, w2)

    def _L1_attn_ref(x, Wqkv, Wproj, bproj):
        import jax, jax.numpy as jnp
        import numpy as np
        N_HEADS = 16
        SCALE = 8.0
        b, n, _ = x.shape
        qkv = jnp.einsum('bnm,fm->bnf', x, Wqkv)
        qkv = qkv.reshape(b, n, N_HEADS, -1)
        dh = qkv.shape[3] // 3
        q, k, v = (qkv[..., :dh], qkv[..., dh:2 * dh], qkv[..., 2 * dh:])
        scores = jnp.einsum('bnhd,bngd->bnhg', q, k) / SCALE
        attn = jax.nn.softmax(scores, axis=-1)
        out = jnp.einsum('bnhg,bngd->bnhd', attn, v)
        out = out.reshape(b, n, -1)
        return jnp.einsum('bni,mi->bnm', out, Wproj) + bproj

    def _L1_xattn_ref(q, k, v, attention_mask, Wq, bq, Wk, bk, Wv, bv, Wo, bo):
        import jax, jax.numpy as jnp
        import numpy as np
        N_HEADS = 16
        D_MODEL = 128
        HEAD_DIM = D_MODEL // N_HEADS
        MASK_FILL = -100000000.0

        def _split_heads(x):
            B, S, _ = x.shape
            return x.reshape(B, S, N_HEADS, HEAD_DIM).transpose(0, 2, 1, 3)
        qm = _split_heads(q @ Wq.T + bq)
        km = _split_heads(k @ Wk.T + bk)
        vm = _split_heads(v @ Wv.T + bv)
        scores = jnp.einsum('bnlh,bnph->bnlp', qm, km) / np.sqrt(HEAD_DIM).astype(np.float32)
        mask = attention_mask[:, None, None, :]
        scores = jnp.where(mask, scores, MASK_FILL)
        attn = jax.nn.softmax(scores, axis=-1)
        out = jnp.einsum('bnlp,bnph->bnlh', attn, vm)
        B, _, L, _ = out.shape
        out = out.transpose(0, 2, 1, 3).reshape(B, L, D_MODEL)
        return out @ Wo.T + bo

    def _L1_ffn_ref(x, router_w, gate_w, up_w, down_w):
        import math
        import jax, jax.numpy as jnp
        from jax import lax
        import numpy as np
        E = 16
        K = 2
        CF = 1.25
        B, S, D = x.shape
        xf = x.reshape(-1, D)
        T = B * S
        capacity = max(1, math.ceil(T * K / E * CF))
        Cbuf = K * capacity
        logits = xf @ router_w
        probs = jax.nn.softmax(logits, axis=-1)
        w, idx = lax.top_k(probs, K)
        oh = jax.nn.one_hot(idx, E, dtype=w.dtype)
        rank = jnp.cumsum(oh, axis=0) - oh
        myrank = jnp.sum(rank * oh, axis=-1)
        keep = myrank < capacity
        w = jnp.where(keep, w, 0.0)
        flat_e = idx.reshape(-1)
        flat_w = w.reshape(-1)
        keep_f = keep.reshape(-1)
        tok = jnp.repeat(jnp.arange(T, dtype=jnp.int32), K)
        ohk = jax.nn.one_hot(flat_e, E, dtype=jnp.int32) * keep_f[:, None].astype(jnp.int32)
        pos = jnp.cumsum(ohk, axis=0) - ohk
        slot = jnp.sum(pos * ohk, axis=-1)
        e_idx = jnp.where(keep_f, flat_e, E)
        dispatch = jnp.full((E + 1, Cbuf), T, dtype=jnp.int32).at[e_idx, slot].set(tok)
        wbuf = jnp.zeros((E + 1, Cbuf), dtype=w.dtype).at[e_idx, slot].set(flat_w)
        dispatch = dispatch[:E]
        wbuf = wbuf[:E]
        x_pad = jnp.concatenate([xf, jnp.zeros((1, D), xf.dtype)], axis=0)
        xe = x_pad[dispatch]
        gate = jnp.einsum('ecd,edh->ech', xe, gate_w)
        up = jnp.einsum('ecd,edh->ech', xe, up_w)
        hidden = jax.nn.silu(gate) * up
        out = jnp.einsum('ech,ehd->ecd', hidden, down_w)
        out = out * wbuf[:, :, None]
        combined = jnp.zeros((T + 1, D), dtype=xf.dtype).at[dispatch.reshape(-1)].add(out.reshape(-1, D))
        return combined[:T].reshape(B, S, D)

    def _L2_attn_ref(x, W_qkv, W_o):
        import math
        import jax, jax.numpy as jnp
        import numpy as np
        D = 128
        NH = 16
        DH = D // NH

        def _rope(q, k, base=10000.0):
            half = q.shape[-1] // 2
            freqs = jnp.arange(half, dtype=q.dtype) / half
            theta = 1.0 / base ** freqs
            t = jnp.arange(q.shape[-2], dtype=q.dtype)
            ang = t[:, None] * theta[None, :]
            cos = jnp.cos(ang)[None, None, :, :]
            sin = jnp.sin(ang)[None, None, :, :]

            def rot(x):
                x1, x2 = (x[..., :half], x[..., half:])
                return jnp.concatenate([x1 * cos - x2 * sin, x1 * sin + x2 * cos], axis=-1)
            return (rot(q), rot(k))
        B, T, d = x.shape
        qkv = x @ W_qkv
        q, k, v = jnp.split(qkv, 3, axis=-1)
        q = q.reshape(B, T, NH, DH).transpose(0, 2, 1, 3)
        k = k.reshape(B, T, NH, DH).transpose(0, 2, 1, 3)
        v = v.reshape(B, T, NH, DH).transpose(0, 2, 1, 3)
        q, k = _rope(q, k)
        att = jnp.einsum('bhtd,bhsd->bhts', q, k) / math.sqrt(DH)
        mask = jnp.triu(jnp.full((T, T), -jnp.inf, dtype=att.dtype), 1)
        att = att + mask
        w = jax.nn.softmax(att, axis=-1)
        y = jnp.einsum('bhts,bhsd->bhtd', w, v)
        y = y.transpose(0, 2, 1, 3).reshape(B, T, d)
        return y @ W_o

    def _L2_xattn_ref(key, query, value, mask, Wq, Wk, Wv, Wo, bo):
        import jax, jax.numpy as jnp
        import numpy as np
        B, S, E, H = (2, 256, 128, 16)
        D = E // H
        Bq, Sq, _ = query.shape
        Sk = key.shape[1]
        k = key.reshape(Bq, Sk, H, D)
        q = query.reshape(Bq, Sq, H, D)
        v = value.reshape(Bq, Sk, H, D)
        q = jnp.einsum('bshd,ed->bhse', q, Wq)
        k = jnp.einsum('bshd,ed->bhse', k, Wk)
        v = jnp.einsum('bshd,ed->bhse', v, Wv)
        product = jnp.einsum('bhqd,bhkd->bhqk', q, k)
        product = jnp.where(mask == 0, jnp.float32(-1e+20), product)
        product = product / jnp.sqrt(jnp.float32(D))
        scores = jax.nn.softmax(product, axis=-1)
        ctx = jnp.einsum('bhqk,bhkd->bhqd', scores, v)
        concat = ctx.transpose(0, 2, 1, 3).reshape(Bq, Sq, H * D)
        return concat @ Wo.T + bo

    def _L2_ffn_ref(x, w1_w, w1_s, w2_w, w2_s, h1_w, h1_s, h2_w, h2_s, w3_w, w3_s):
        import jax, jax.numpy as jnp
        import numpy as np
        D_IN, D_HID = (128, 512)

        def _ternary(key, shape):
            return jax.random.randint(key, shape, -1, 2).astype(jnp.float32)

        def _tlin(x, w, s):
            return jnp.einsum('bsi,oi->bso', x, w) * s
        h = jax.nn.silu(_tlin(x, w1_w, w1_s)) * _tlin(x, w2_w, w2_s)
        h = jax.nn.gelu(_tlin(h, h1_w, h1_s), approximate=False)
        h = jax.nn.gelu(_tlin(h, h2_w, h2_s), approximate=False)
        return _tlin(h, w3_w, w3_s)

    def _L3_attn_ref(x, W, b):
        import jax, jax.numpy as jnp
        import numpy as np
        MAX_DISTANCE = 10
        SCALE = 0.01

        def distance_bias(seq_len):
            idx = jnp.arange(seq_len, dtype=jnp.float32)
            d = jnp.abs(idx[None, :] - idx[:, None])
            return jnp.clip(d, 0.0, MAX_DISTANCE) * SCALE
        B, S, _ = x.shape
        f = x @ W + b
        e = jnp.einsum('bsd,btd->bst', f, f)
        e = e + distance_bias(S)[None, :, :]
        a = jax.nn.softmax(e, axis=-1)
        out = jnp.einsum('bst,btd->bsd', a, f)
        return out

    def _L3_xattn_ref(query, key, value, Wq, bq, Wk, bk, Wv, bv, Wo, bo):
        import jax, jax.numpy as jnp
        import numpy as np
        EMBED_DIM = 128
        NUM_HEADS = 16
        HEAD_DIM = EMBED_DIM // NUM_HEADS
        B, L = (4, 256)
        NEG_INF = jnp.float32(-1e+30)

        def _split_heads(x):
            b, l, _ = x.shape
            return x.reshape(b, l, NUM_HEADS, HEAD_DIM).transpose(0, 2, 1, 3)
        q = _split_heads(query @ Wq.T + bq)
        k = _split_heads(key @ Wk.T + bk)
        v = _split_heads(value @ Wv.T + bv)
        scores = jnp.einsum('bhqd,bhkd->bhqk', q, k) / np.sqrt(HEAD_DIM)
        q_len, k_len = (query.shape[1], key.shape[1])
        causal = jnp.triu(jnp.ones((q_len, k_len), jnp.bool_), k=1)
        scores = jnp.where(causal[None, None], NEG_INF, scores)
        attn = jax.nn.softmax(scores, axis=-1)
        out = jnp.einsum('bhqk,bhkd->bhqd', attn, v)
        out = out.transpose(0, 2, 1, 3).reshape(query.shape[0], q_len, EMBED_DIM)
        return out @ Wo.T + bo

    def _L3_ffn_ref(x, Wg, Wu, Wd, Wr, temperature):
        import jax, jax.numpy as jnp
        import numpy as np
        import math
        GOLDEN_CENTER = 1.0 / math.e
        GOLDEN_LOWER = 0.5 - math.log(4.0 / 3.0)
        GOLDEN_UPPER = 0.5
        B, T, D = (4, 256, 128)
        E = 8
        I = 512 // (E // 2)

        def _routing_weights(x, Wr, temperature):
            inh = jax.nn.sigmoid(x @ Wr / temperature)
            in_zone = (inh >= GOLDEN_LOWER) & (inh <= GOLDEN_UPPER)
            dist = jnp.abs(inh - GOLDEN_CENTER)
            w = jnp.exp(-dist / 0.1) * in_zone.astype(x.dtype)
            wsum = w.sum(axis=-1, keepdims=True)
            no_expert = wsum < 1e-08
            fb = jnp.exp(-dist / 0.3)
            _, top2 = jax.lax.top_k(fb, 2)
            fb_mask = jax.nn.one_hot(top2, E, dtype=x.dtype).sum(axis=-2)
            fb_w = fb * fb_mask
            fb_w = fb_w / jnp.clip(fb_w.sum(axis=-1, keepdims=True), 1e-08)
            w = jnp.where(no_expert, fb_w, w)
            wsum = w.sum(axis=-1, keepdims=True)
            return w / jnp.clip(wsum, 1e-08)
        weights = _routing_weights(x, Wr, temperature)
        gate = jnp.einsum('btd,edi->beti', x, Wg)
        up = jnp.einsum('btd,edi->beti', x, Wu)
        h = jax.nn.silu(gate) * up
        e_out = jnp.einsum('beti,eid->betd', h, Wd)
        out = jnp.einsum('bte,betd->btd', weights, e_out)
        return out
    x = _layernorm(x + _L0_attn_ref(x, L0_attn_Wq, L0_attn_bq, L0_attn_Wk, L0_attn_bk, L0_attn_Wv, L0_attn_bv, L0_attn_Wo, L0_attn_bo), axis=-1)
    x = _layernorm(x + _L0_xattn_ref(x, ctx_1024, ctx_1024, L0_xattn_w_q, L0_xattn_b_q, L0_xattn_w_k, L0_xattn_b_k, L0_xattn_w_v, L0_xattn_b_v, L0_xattn_w_out, L0_xattn_b_out), axis=-1)
    x = _layernorm(x + _L0_ffn_ref(x, L0_ffn_w1, L0_ffn_conv_w, L0_ffn_conv_b, L0_ffn_w2), axis=-1)
    x = _layernorm(x + _L1_attn_ref(x, L1_attn_Wqkv, L1_attn_Wproj, L1_attn_bproj), axis=-1)
    x = _layernorm(x + _L1_xattn_ref(x, ctx_1024, ctx_1024, mask_BxS2_bf1, L1_xattn_Wq, L1_xattn_bq, L1_xattn_Wk, L1_xattn_bk, L1_xattn_Wv, L1_xattn_bv, L1_xattn_Wo, L1_xattn_bo), axis=-1)
    x = _layernorm(x + _L1_ffn_ref(x, L1_ffn_router_w, L1_ffn_gate_w, L1_ffn_up_w, L1_ffn_down_w), axis=-1)
    x = _layernorm(x + _L2_attn_ref(x, L2_attn_W_qkv, L2_attn_W_o), axis=-1)
    x = _layernorm(x + _L2_xattn_ref(ctx_1024, x, ctx_1024, mask_1x1xSxS2_bk0, L2_xattn_Wq, L2_xattn_Wk, L2_xattn_Wv, L2_xattn_Wo, L2_xattn_bo), axis=-1)
    x = _layernorm(x + _L2_ffn_ref(x, L2_ffn_w1_w, L2_ffn_w1_s, L2_ffn_w2_w, L2_ffn_w2_s, L2_ffn_h1_w, L2_ffn_h1_s, L2_ffn_h2_w, L2_ffn_h2_s, L2_ffn_w3_w, L2_ffn_w3_s), axis=-1)
    x = _layernorm(x + _L3_attn_ref(x, L3_attn_W, L3_attn_b), axis=-1)
    x = _layernorm(x + _L3_xattn_ref(x, ctx_1024, ctx_1024, L3_xattn_Wq, L3_xattn_bq, L3_xattn_Wk, L3_xattn_bk, L3_xattn_Wv, L3_xattn_bv, L3_xattn_Wo, L3_xattn_bo), axis=-1)
    x = _layernorm(x + _L3_ffn_ref(x, L3_ffn_Wg, L3_ffn_Wu, L3_ffn_Wd, L3_ffn_Wr, L3_ffn_temperature), axis=-1)
    return x

_drawn_inputs = setup_inputs


def setup_inputs(seed=0):
    import zlib

    import numpy as np

    out = dict(_drawn_inputs(seed))
    spreads = {'L0_attn_bq': (0.0, 0.582),
     'L0_attn_bk': (0.0, 0.1),
     'L0_attn_bv': (0.0, 0.8),
     'L0_attn_bo': (0.0, 0.1),
     'L0_xattn_b_q': (0.0, 0.1),
     'L0_xattn_b_k': (0.0, 0.8),
     'L0_xattn_b_v': (0.0, 0.1),
     'L0_xattn_b_out': (0.0, 0.1),
     'L1_xattn_bq': (0.0, 0.1),
     'L1_xattn_bk': (0.0, 0.8),
     'L1_xattn_bv': (0.0, 0.1),
     'L1_xattn_bo': (0.0, 0.1),
     'L3_attn_b': (0.0, 0.1)}
    factors = {'L1_ffn_router_w': 5.233,
     'L1_ffn_gate_w': 7.942,
     'L1_ffn_up_w': 8.0,
     'L1_ffn_down_w': 8.0,
     'L2_ffn_w1_w': 4.108,
     'L2_ffn_w1_s': 3.871,
     'L2_ffn_w2_w': 3.347,
     'L2_ffn_w2_s': 4.734,
     'L2_ffn_h1_w': 4.423,
     'L2_ffn_h1_s': 6.063,
     'L2_ffn_h2_w': 3.33,
     'L2_ffn_h2_s': 5.621,
     'L2_ffn_w3_w': 3.732,
     'L2_ffn_w3_s': 4.594,
     'L3_xattn_bq': 4.491,
     'L3_xattn_bk': 8.0}
    for name, (base, spread) in spreads.items():
        noise = np.random.default_rng([zlib.crc32(name.encode()), seed]).standard_normal(out[name].shape)
        drawn = base * np.exp(spread * noise) if base else spread * noise
        out[name] = jnp.asarray(drawn.astype(out[name].dtype))
    for name, factor in factors.items():
        out[name] = (out[name] * factor).astype(out[name].dtype)
    return out
```

```python
from contextlib import ExitStack
from dataclasses import dataclass

import numpy as np
import concourse.bass as bass
from concourse import mybir

ALU = mybir.AluOpType
ACT = mybir.ActivationFunctionType
AX = mybir.AxisListType
F32 = mybir.dt.float32
BF16 = mybir.dt.bfloat16
U8 = mybir.dt.uint8
U32 = mybir.dt.uint32

B, S, D, H, DH = 4, 512, 128, 16, 8
KC, KP = 154, 160
REM = KC - 128
QT = S // 128
FC = 4
NE, NE3 = 16, 8
CAP = -(-B * S * 2 * 5 // (NE * 4))
MAGIC = 1.5 * 2.0 ** 23
GOLD = 1.0 / np.e
GOLD_LOW, GOLD_HIGH = 0.5 - float(np.log(4.0 / 3.0)), 0.5
PIECES_Q = [(0, 3, 0, True), (3, 2, 1, True), (5, 1, 2, True)]
PIECES_K = [(0, 3, 0, False), (3, 2, 0, False), (5, 1, 0, True)]
ROW_M, ROW_MASK = 48, 51

PACK = [
    ("ident", 128), ("center", 128), ("mean", 128), ("eps", 1), ("zero", 1),
    ("L0a.wq", 128), ("L0a.wq_rot", 128), ("L0a.wk", 128), ("L0a.wk_rot", 128), ("L0a.wv", 128), ("L0a.wo", 128),
    ("L0a.bq", 1), ("L0a.bq_rot", 1), ("L0a.bk", 1), ("L0a.bk_rot", 1), ("L0a.bv", 1), ("L0a.bo", 1),
    ("split", 0),
    ("L0x.wq", 128), ("L0x.wk", 128), ("L0x.wv", 128), ("L0x.wo", 128), ("L0x.bq", 1), ("L0x.bk", 1), ("L0x.bv", 1), ("L0x.bo", 1),
    ("f0.w1", 512), ("f0.w2", 512), ("f0.taps", 12), ("f0.bias", 4),
    ("L1a.wqkv", 384), ("L1a.wo", 128), ("L1a.bo", 1),
    ("L1x.wq", 128), ("L1x.wk", 128), ("L1x.wv", 128), ("L1x.wo", 128), ("L1x.bq", 1), ("L1x.bk", 1), ("L1x.bv", 1), ("L1x.bo", 1),
    ("f1.router", NE), ("iota", NE),
    ("L2a.wq", 128), ("L2a.wq_rot", 128), ("L2a.wk", 128), ("L2a.wk_rot", 128), ("L2a.wv", 128), ("L2a.wo", 128),
    ("L2x.wq", 128), ("L2x.wk", 128), ("L2x.wv", 128), ("L2x.wo", 128), ("L2x.bo", 1),
    ("f2.s1", 4), ("f2.s2", 4), ("f2.sh1", 4), ("f2.sh2", 4), ("f2.s3", 1),
    ("L3a.w", 128), ("L3a.b", 1),
    ("L3x.wq", 128), ("L3x.wk", 128), ("L3x.wv", 128), ("L3x.wo", 128), ("L3x.bq", 1), ("L3x.bk", 1), ("L3x.bv", 1), ("L3x.bo", 1),
    ("f3.router", NE3), ("f3.temperature", 1),
]
AT, _at = {}, 0
for _name, _width in PACK:
    AT[_name] = (_at, _width)
    _at += _width
NPACK = _at
WIDE = [("f2.w1", 512), ("f2.w2", 512), ("f2.h1", 2048), ("f2.h2", 2048), ("f2.w3", 512)]
WAT, _at = {}, 0
for _name, _width in WIDE:
    WAT[_name] = (_at, _width)
    _at += _width
NWIDE = _at
CONST = [("ident", 128), ("tri_qk", 128), ("tri_kq", 128), ("rep", 128), ("lower", 128), ("ones", 128),
         ("mq3", 320), ("mr3", 256), ("band", 1152)]
CAT, _at = {}, 0
for _name, _width in CONST:
    CAT[_name] = (_at, _width)
    _at += _width
NCONST = _at

@dataclass
class Cfg:
    name: str
    cross: bool
    rope: bool
    causal: bool
    scale: float
    mask: str


LAYERS = [
    Cfg(name="L0a", cross=False, rope=True, causal=True, scale=1.0, mask=""),
    Cfg(name="L0x", cross=True, rope=False, causal=False, scale=8 ** -0.5, mask=""),
    Cfg(name="L1x", cross=True, rope=False, causal=False, scale=8 ** -0.5, mask="keys"),
    Cfg(name="L2a", cross=False, rope=True, causal=True, scale=1.0, mask=""),
    Cfg(name="L2x", cross=True, rope=False, causal=False, scale=8 ** -0.5, mask="full"),
    Cfg(name="L3x", cross=True, rope=False, causal=False, scale=8 ** -0.5, mask="causal"),
]
GROUPS = [[0, 1], [2], [3, 4], [5]]


def pre_fills(L):
    return 5 if L.rope else 3


def max_units(L):
    if L.cross:
        return [(i, min(3, H * QT - i)) for i in range(0, H * QT, 3)]
    return [(i, 1) for i in range(H * QT)]


def pair_units(L):
    if not L.cross:
        return [("full", g, kt, jj) for g in range(4) for kt in range(QT) for jj in range(2)]
    out = []
    for gp in range(2):
        out.append(("rem", gp))
        out += [("full", g, 0, jj) for g in (2 * gp, 2 * gp + 1) for jj in range(2)]
    return out


def value_blocks(L):
    units = pair_units(L)
    out = []
    for n, u in enumerate(units):
        if u[0] == "full" and u[3] == 1:
            if L.cross:
                rem = units.index(("rem", u[1] // 2))
                out.append((n, u[1], 0, True, True, (n - 1, n), rem))
            else:
                out.append((n, u[1], u[2], u[2] == 0, u[2] == QT - 1, (n - 1, n), None))
    return out


SETUP_DONE = 8
NSLOT = 6
FRONTS = [(li, b) for grp in GROUPS for li in grp for b in range(B)]
FILL_BASE, PAIR_BASE, BLOCK_BASE = [0], [0], [0]
for _li, _b in FRONTS:
    FILL_BASE.append(FILL_BASE[-1] + pre_fills(LAYERS[_li]) + len(max_units(LAYERS[_li])) + 1)
    PAIR_BASE.append(PAIR_BASE[-1] + len(pair_units(LAYERS[_li])))
    BLOCK_BASE.append(BLOCK_BASE[-1] + len(value_blocks(LAYERS[_li])))
OPERAND_DMAS = [0]
for _F, (_li, _b) in enumerate(FRONTS):
    OPERAND_DMAS.append(OPERAND_DMAS[-1] + 13 + (LAYERS[_li].mask == "keys" or (LAYERS[_li].name == "L2a" and _b < 2)))
LAST_READER = {}
for _F, (_li, _b) in enumerate(FRONTS):
    for _k, _blk in enumerate(value_blocks(LAYERS[_li])):
        for _n in _blk[5] + (() if _blk[6] is None else (_blk[6],)):
            LAST_READER[PAIR_BASE[_F] + _n] = BLOCK_BASE[_F] + _k
STAGES = [("attn", 0), ("ffn", 0), ("heads", 1), ("attn", 1), ("ffn", 1), ("attn", 2), ("ffn", 2), ("self3", 0), ("attn", 3), ("ffn", 3)]
TAILS = []
for _kind, _i in STAGES:
    if _kind == "attn":
        TAILS += [("attn", F) for F, (li, b) in enumerate(FRONTS) if li in GROUPS[_i]]
    else:
        TAILS += [(f"{_kind}{_i}", b) for b in range(B)]
TAIL_OF = {t: n for n, t in enumerate(TAILS)}
MISC_BASE = [0]
for _t in TAILS:
    MISC_BASE.append(MISC_BASE[-1] + (8 if _t[0] == "attn" else 3))
STAGE_FIRST = {}
_n = 0
for _kind, _i in STAGES:
    STAGE_FIRST[(_kind, _i)] = _n
    _n += B * len(GROUPS[_i]) if _kind == "attn" else B


def program(nc, d, out):
    with ExitStack() as ctx:
        def sb(name, shape, dt=F32):
            return ctx.enter_context(nc.sbuf_tensor(name, shape, dt))

        sems = {}

        def sem(name):
            if name not in sems:
                sems[name] = ctx.enter_context(nc.semaphore(name))
            return sems[name]

        pack = sb("pack", [128, NPACK])
        const = sb("const", [128, NCONST], BF16)
        XT = sb("XT", [128, B, S])
        CT = sb("CT", [128, B, KP])
        tables = sb("tables", [128, 4, S])
        QH = [sb(f"QH{i}", [128, H, S], BF16) for i in range(2)]
        KH = [sb(f"KH{i}", [128, H, S], BF16) for i in range(2)]
        VA = [sb(f"VA{i}", [128, QT, H, 32]) for i in range(2)]
        WORK = sb("WORK", [128, 21 * S])

        def part(at, n):
            return WORK[:, at * S:(at + n) * S]
        PB = part(0, 12).rearrange("p (n i s) -> p n i s", n=NSLOT, i=2)
        US = part(12, 4).rearrange("p (g s) -> p g s", g=4)
        TQ, TK, TR, RQ, RK = (part(16 + i, 1) for i in range(5))
        HQ, HK = sb("HQ", [128, 3, S], BF16), sb("HK", [128, 3, S], BF16)
        MX = sb("MX", [128, H * QT])
        MR = sb("MR", [128, H * QT])
        MP = sb("MP", [128, QT, 3, H], BF16)
        MT = sb("MT", [48, S], BF16)
        RD = sb("RD", [128, QT * 4])
        OK = sb("OK", [128, QT, D])
        OT, YT, YC, SQ, RS = (sb(n, [128, S]) for n in ("OT", "YT", "YC", "SQ", "RS"))
        LV = SQ
        BO = sb("BO", [128, 7])
        MQ2 = sb("MQ2", [128, QT, KP], BF16)
        MT2 = sb("MT2", [128, S], BF16)
        MR2 = sb("MR2", [128, S], BF16)
        MU = sb("MU", [128, QT * KP], U8)
        MU2 = sb("MU2", [128, S], U8)
        MU3 = sb("MU3", [32, S], U8)
        MU4 = sb("MU4", [128, B * KP], U8)
        MF = sb("MF", [128, B, KP])
        MK = sb("MK", [3, H, KP], BF16)
        MKF = sb("MKF", [3, KP])
        mconst = sb("mconst", [3, 1])
        ps = ctx.enter_context(nc.psum_tensor("ps", [128, 8, S], F32))
        scratch = nc.dram_tensor("scratch", (2, 2, 3, D, S), BF16, kind="Internal").ap()
        mscratch = nc.dram_tensor("mscratch", (2, 3 * H, S), BF16, kind="Internal").ap()

        WQ1, WQ2 = part(0, 1), part(1, 1)
        XQ = part(2, 1).rearrange("p (t d) -> p t d", t=QT)
        XQT = part(3, 1)
        HC, HS, HQT = (part(4 + 4 * i, 4).rearrange("p (c s) -> p c s", c=FC) for i in range(3))
        HR = part(16, 1)
        W0S, W0M, W0R = (part(17, 1)[:, 2 * i:2 * i + 2] for i in range(3))
        AM, SC, IV = (part(17, 1)[:, 8 * i + 8:8 * i + 16] for i in range(3))
        QKV1 = [part(i, 1)[:, 0:384].rearrange("p (w h e) -> p w h e", w=3, h=H) for i in range(2)]
        PR1, PV1 = ([part(2 + 8 * i + 4 * k, 4) for k in range(2)] for i in range(2))
        SC1 = [part(18, 1)[:, i * 256:(i + 1) * 256].rearrange("p (h g) -> p h g", h=H) for i in range(2)]
        MH1 = [part(19, 1)[:, 16 * i:16 * i + 16] for i in range(2)]
        RH1 = [part(19, 1)[:, 32 + 16 * i:48 + 16 * i] for i in range(2)]
        OH1 = [part(19, 1)[:, 128 + 128 * i:256 + 128 * i].rearrange("p (h e) -> p h e", h=H) for i in range(2)]
        OT1 = part(20, 1)
        EW = [part(0, 2)[:, i * 384:(i + 1) * 384] for i in range(2)]
        HID = [part(2 + i, 1) for i in range(2)]
        SG = [part(4 + i, 1) for i in range(2)]
        ACC = part(6, 4).rearrange("p (b t d) -> p b t d", b=B, t=QT)
        WC, E16 = (part(10, 1)[:, i * 256:(i + 1) * 256].rearrange("p (n e) -> p n e", e=NE) for i in range(2))
        OHF = part(11, 1).rearrange("p (n k e) -> p n k e", k=2, e=NE)
        OHB, OHS = (part(12, 1).bitcast(BF16)[:, i * 512:(i + 1) * 512].rearrange("p (n e) -> p n e", e=2 * NE)
                    for i in range(2))
        T8, I8F = (part(13, 1)[:, i * 128:(i + 1) * 128].rearrange("p (n e) -> p n e", e=8) for i in range(2))
        I8 = part(14, 1)[:, 0:128].bitcast(U32).rearrange("p (n e) -> p n e", e=8)
        RM = part(14, 1)[:, 128:144]
        R3 = [part(15, 1)[:, i * 128:(i + 1) * 128].rearrange("p (n e) -> p n e", e=NE3) for i in range(4)]
        WW = part(0, 11)
        SG2 = [part(11 + i, 1) for i in range(2)]
        G0, G1 = (part(13 + 4 * i, 4).rearrange("p (c s) -> p c s", c=FC) for i in range(2))
        FT3 = part(0, 1)
        FK3 = part(1, 1).rearrange("p (t d) -> p t d", t=QT)
        P3, PT3 = (part(2 + 4 * i, 4).rearrange("p (t s) -> p t s", t=QT) for i in range(2))
        M3, L3S, L3R = (part(10, 1)[:, i * 16:(i + 1) * 16] for i in range(3))
        OUT = part(0, 4).rearrange("p (b t d) -> p b t d", b=B, t=QT)

        def WWIDE(name, lo, n):
            return WW[:, WAT[name][0] + lo:WAT[name][0] + lo + n]

        def W(name, lo=0, n=None):
            a, w = AT[name]
            return pack[:, a + lo:a + (w if n is None else lo + n)]

        def C(name, lo=0, n=None):
            a, w = CAT[name]
            return const[:, a + lo:a + (w if n is None else lo + n)]

        RING, EXPB, UB, MISC = 0, 2, 6, 7
        block = ctx.enter_context(nc.Block())

        def tail_x(stage_i, b):
            return stage_i - B + b + 1

        def x_ready(eng, first_tail, b):
            if first_tail >= B:
                eng.wait_ge(sem("x_done"), tail_x(first_tail, b))
            else:
                eng.wait_ge(sem("x_loaded"), 16)

        def layer_first_tail(F):
            return TAIL_OF[("attn", F - FRONTS[F][1])]

        def steps(grp):
            first = FRONTS.index((GROUPS[grp][0], 0))
            n = B * len(GROUPS[grp])
            for s in range(n + 2):
                yield tuple(first + s - lag if 0 <= s - lag < n else None for lag in range(3))

        def follows(front):
            if front is None or front + 1 == len(FRONTS):
                return None
            same = [g for g in GROUPS if FRONTS[front][0] in g and FRONTS[front + 1][0] in g]
            return front + 1 if same else None

        def loop_of(front, back):
            nf = len(max_units(LAYERS[FRONTS[front][0]])) if front is not None else 0
            nb = len(pair_units(LAYERS[FRONTS[back][0]])) if back is not None else 0
            n = max(10, nb, nf // 2)
            lo, hi = n * 2 // 10 if nb else 0, n * 7 // 10
            w = hi - lo
            for p in range(n):
                fu = range((p - lo) * nf // w, (p - lo + 1) * nf // w) if lo <= p < hi else range(0)
                phases = [name for name, at in (("split", hi), ("turn", hi + n // 10), ("project", min(n - 1, hi + n // 10 + 1)))
                          if at == p and front is not None]
                yield p, fu, range(p * nb // n, (p + 1) * nb // n), phases

        TAIL_AT = {p + 1: p for p in range(8)}

        @block.tensor
        def _(pe):
            filled, freed = sem("ring_filled"), sem("ring_freed")

            def ring(n):
                if n >= 2:
                    pe.wait_ge(freed, n - 1)
                return ps[:, RING + n % 2, :]

            def front_projections(F):
                li, b = FRONTS[F]
                L = LAYERS[li]
                n = FILL_BASE[F]
                x = XT[:, b, :]
                src = CT[:, b, :] if L.cross else x
                nk = KP if L.cross else S
                names = [("wq", x, S)] + ([("wq_rot", x, S)] if L.rope else [])
                names += [("wk", src, nk)] + ([("wk_rot", src, nk)] if L.rope else [])
                x_ready(pe, layer_first_tail(F), b)
                for name, rhs, width in names:
                    bank = ring(n)
                    pe.matmul(bank[:, 0:width], W(f"{L.name}.{name}"), rhs, start=True, stop=True).then_inc(filled, 1)
                    n += 1
                bank = ring(n)
                wv = W(f"{L.name}.wv")
                if L.cross:
                    pe.matmul(bank[:, 0:128], src[:, 0:128], wv, start=True, stop=True)
                    for j in range(4):
                        mm = pe.matmul(bank[32 * j:32 * j + 32, 128:256], src[:, 128:160], wv, start=True, stop=True,
                                       skip_group_check=True)
                else:
                    for t in range(QT):
                        mm = pe.matmul(bank[:, t * 128:t * 128 + 128], src[:, t * 128:t * 128 + 128], wv,
                                       start=True, stop=True, skip_group_check=True)
                mm.then_inc(filled, 1)

            def max_unit(F, u):
                L = LAYERS[FRONTS[F][0]]
                par = F % 2
                if u == 0:
                    pe.wait_ge(sem("operands_loaded"), OPERAND_DMAS[F + 1] * 16)
                bank = ring(FILL_BASE[F] + pre_fills(L) + u)
                i0, cnt = max_units(L)[u]
                for c in range(cnt):
                    h, t = divmod(i0 + c, QT)
                    q = QH[par][:, h, t * 128:t * 128 + 128]
                    if L.cross:
                        o = bank[:, c * KP:c * KP + KC]
                        masked = L.mask == "full" or (L.mask == "causal" and t < 2)
                        mm = pe.matmul(o, q, KH[par][:, h, 0:KC], start=(c == 0), stop=not masked, skip_group_check=True)
                        if masked:
                            m = MQ2[:, t, 0:KC] if L.mask == "full" else C("mq3", t * KP, KC)
                            mm = pe.matmul(o, C("ident"), m, start=False, stop=True, skip_group_check=True)
                    else:
                        n = 128 * (t + 1) if L.causal else S
                        mm = pe.matmul(bank[:, 0:n], q, KH[par][:, h, 0:n], start=True, stop=not L.causal)
                        if L.causal:
                            mm = pe.matmul(bank[:, n - 128:n], C("ident"), C("tri_qk"), start=False, stop=True)
                mm.then_inc(filled, 1)

            def turn_maxima(F):
                L = LAYERS[FRONTS[F][0]]
                bank = ring(FILL_BASE[F + 1] - 1).bitcast(BF16)
                pe.wait_ge(sem("maxima_split"), F + 1)
                for t in range(QT):
                    mm = pe.transpose(bank[0:48, t * 128:t * 128 + 128], MP[:, t, :, :].rearrange("p a h -> p (a h)"),
                                      C("ident"))
                mm.then_inc(filled, 1)

            def exp_pair(F, n):
                L = LAYERS[FRONTS[F][0]]
                par, N = F % 2, PAIR_BASE[F] + n
                if n == 0:
                    pe.wait_ge(sem("maxima_loaded"), 16 * (F + 1))
                if N >= 2:
                    pe.wait_ge(sem("exp_done"), N - 1)
                bank = ps[:, EXPB + 2 * (N % 2):EXPB + 2 * (N % 2) + 2, :]
                u = pair_units(L)[n]
                if u[0] == "full":
                    _, g, kt, jj = u
                    for i in range(2):
                        h = 4 * g + 2 * jj + i
                        q0 = 128 * kt if L.causal else 0
                        masked = L.causal or L.mask in ("full", "causal")
                        mm = pe.matmul(bank[:, i, q0:S], KH[par][:, h, kt * 128:kt * 128 + 128], QH[par][:, h, q0:S],
                                       start=True, stop=not masked)
                        if L.mask == "full":
                            mm = pe.matmul(bank[:, i, :], C("ident"), MT2[:], start=False, stop=True)
                        elif masked:
                            mm = pe.matmul(bank[:, i, q0:q0 + 128], C("ident"), C("tri_kq"), start=False, stop=True)
                else:
                    for i in range(2):
                        for j in range(4):
                            h = 4 * (2 * u[1] + i) + j
                            mm = pe.matmul(bank[32 * j:32 * j + 32, i, :], KH[par][:, h, 128:160], QH[par][:, h, :],
                                           start=True, stop=L.mask not in ("full", "causal"), skip_group_check=True)
                        if L.mask == "full":
                            mm = pe.matmul(bank[:, i, :], C("rep"), MR2[:], start=False, stop=True, skip_group_check=True)
                        elif L.mask == "causal":
                            mm = pe.matmul(bank[:, i, 0:256], C("rep"), C("mr3"), start=False, stop=True,
                                           skip_group_check=True)
                mm.then_inc(sem("scores_ready"), 1)

            def value_block(F, k):
                L = LAYERS[FRONTS[F][0]]
                par = F % 2
                last, g, kt, first, stops, pairs, rem = value_blocks(L)[k]
                pe.wait_ge(sem("exp_done"), PAIR_BASE[F] + last + 1)
                if first and 4 * F + g >= 1:
                    pe.wait_ge(sem("outputs_copied"), 4 * F + g)
                q0 = 128 * kt if L.causal else 0
                for j in range(4):
                    slot = (PAIR_BASE[F] + pairs[j // 2]) % NSLOT
                    mm = pe.matmul(ps[32 * j:32 * j + 32, UB, q0:S], VA[par][:, kt, 4 * g + j, :],
                                   PB[:, slot, j % 2, q0:S], start=first, stop=stops and rem is None,
                                   skip_group_check=True)
                if rem is not None:
                    slot = (PAIR_BASE[F] + rem) % NSLOT
                    for j in range(4):
                        mm = pe.matmul(ps[32 * j:32 * j + 32, UB, :], VA[par][32 * j:32 * j + REM, 1, 4 * g + j, :],
                                       PB[32 * j:32 * j + REM, slot, g % 2, :], start=False, stop=True,
                                       tile_position=(32 * j, 32 * j), skip_group_check=True)
                mm.then_inc(sem("values_done"), 1)

            def misc(T):
                if T >= 1:
                    pe.wait_ge(sem("x_done"), T)
                return ps[:, MISC, :]

            def tail(T, stage):
                kind, F = TAILS[T]
                bank = ps[:, MISC, :]
                if stage < 4:
                    if stage == 0:
                        misc(T)
                        pe.wait_ge(sem("outputs_copied"), 4 * (F + 1))
                    else:
                        pe.wait_ge(sem("normalised"), 4 * F + stage)
                    for t in range(QT):
                        mm = pe.transpose(bank[:, t * 128:t * 128 + 128], US[:, stage, t * 128:t * 128 + 128], W("ident"))
                elif stage == 4:
                    pe.wait_ge(sem("normalised"), 4 * F + 4)
                    for t in range(QT):
                        mm = pe.transpose(bank[:, t * 128:t * 128 + 128], OK[:, t, :], W("ident"))
                elif stage == 5:
                    pe.wait_ge(sem("outputs_turned"), F + 1)
                    mm = pe.matmul(bank, W(f"{LAYERS[FRONTS[F][0]].name}.wo"), OT[:], start=True, stop=True)
                elif stage == 6:
                    pe.wait_ge(sem("summed"), T + 1)
                    mm = pe.matmul(bank, W("center"), YT[:], start=True, stop=True)
                else:
                    pe.wait_ge(sem("squared"), T + 1)
                    mm = pe.matmul(bank, W("mean"), SQ[:], start=True, stop=True)
                mm.then_inc(sem("misc_filled"), 1)

            def attention(grp):
                front_projections(FRONTS.index((GROUPS[grp][0], 0)))
                for front, back, tl in steps(grp):
                    nb = 0
                    blocks = value_blocks(LAYERS[FRONTS[back][0]]) if back is not None else []
                    for p, fu, bu, phases in loop_of(front, back):
                        for u in bu:
                            exp_pair(back, u)
                            while nb < len(blocks) and blocks[nb][0] <= u - 2:
                                value_block(back, nb)
                                nb += 1
                        for u in fu:
                            max_unit(front, u)
                        if tl is not None and p in TAIL_AT:
                            tail(TAIL_OF[("attn", tl)], TAIL_AT[p])
                        if "turn" in phases:
                            turn_maxima(front)
                        if "project" in phases and follows(front) is not None:
                            front_projections(front + 1)
                    while nb < len(blocks):
                        value_block(back, nb)
                        nb += 1

            def ffn_tail(kind, b):
                tail(TAIL_OF[(kind, b)], 6)
                tail(TAIL_OF[(kind, b)], 7)

            def all_x(first_tail):
                pe.wait_ge(sem("x_done"), first_tail)

            def ffn0():
                all_x(STAGE_FIRST[("ffn", 0)])
                pe.wait_ge(sem("w0_sums"), 2)
                pe.matmul(ps[:, 6, 0:2], W("mean"), W0S, start=True, stop=True).then_inc(sem("w0_means"), 1)
                for b in range(B):
                    pe.wait_ge(sem("x_done"), tail_x(STAGE_FIRST[("ffn", 0)], b))
                    if b:
                        pe.wait_ge(sem("h0_rounded"), QT * b)
                        pe.wait_ge(sem("h0_back_copied"), QT * b)
                    for t in range(QT):
                        mm = pe.transpose(ps[:, 0, t * 128:t * 128 + 128], XT[:, b, t * 128:t * 128 + 128], W("ident"))
                    mm.then_inc(sem("x0_turned"), 1)
                    pe.wait_ge(sem("q0_rounded"), b + 1)
                    for t in range(QT):
                        mm = pe.transpose(ps[:, 1, t * 128:t * 128 + 128], XQ[:, t, :], W("ident"))
                    mm.then_inc(sem("x0_back"), 1)
                    pe.wait_ge(sem("q0_turned"), b + 1)
                    pe.wait_ge(sem("w0_ready"), 2)
                    if b:
                        pe.wait_ge(sem("conv_done"), FC * b)
                    for c in range(FC):
                        pe.matmul(ps[:, 2 + c, :], WQ1[:, c * 128:c * 128 + 128], XQT, start=True, stop=True)\
                            .then_inc(sem("h0_ready"), 1)
                    for t in range(QT):
                        n = b * QT + t
                        pe.wait_ge(sem("silu0_done"), FC * (b + 1))
                        if n:
                            pe.wait_ge(sem("h0_rounded"), n)
                        for c in range(FC):
                            mm = pe.transpose(ps[:, 0, c * 128:c * 128 + 128], HS[:, c, t * 128:t * 128 + 128], W("ident"))
                        mm.then_inc(sem("h0_turned"), 1)
                        pe.wait_ge(sem("h0_rounded"), n + 1)
                        if n:
                            pe.wait_ge(sem("h0_back_copied"), n)
                        for c in range(FC):
                            mm = pe.transpose(ps[:, 1, c * 128:c * 128 + 128], HR[:, c * 128:c * 128 + 128], W("ident"))
                        mm.then_inc(sem("h0_back"), 1)
                    T = TAIL_OF[("ffn0", b)]
                    bank = misc(T)
                    pe.wait_ge(sem("h0_back_copied"), QT * (b + 1))
                    for c in range(FC):
                        mm = pe.matmul(bank, WQ2[:, c * 128:c * 128 + 128], HQT[:, c, :], start=(c == 0), stop=(c == FC - 1))
                    mm.then_inc(sem("misc_filled"), 1)
                    ffn_tail("ffn0", b)

            def heads1():
                all_x(STAGE_FIRST[("heads", 1)])

                def turn(n):
                    b, t = divmod(n, QT)
                    pe.wait_ge(sem("heads1_mixed"), n + 1)
                    if t == 0 and b >= 2:
                        pe.wait_ge(sem("mixed1_copied"), b - 1)
                    pe.transpose(ps[:, 2 + b % 2, t * 128:t * 128 + 128], OH1[n % 2].rearrange("p h e -> p (h e)"),
                                 W("ident")).then_inc(sem("mixed1_turned"), 1)
                    if t == QT - 1:
                        bank = misc(TAIL_OF[("heads1", b)])
                        pe.wait_ge(sem("mixed1_copied"), b + 1)
                        pe.matmul(bank, W("L1a.wo"), OT1, start=True, stop=True).then_inc(sem("misc_filled"), 1)
                        ffn_tail("heads1", b)

                for n in range(B * QT):
                    b, t = divmod(n, QT)
                    if n >= 2:
                        pe.wait_ge(sem("qkv1_copied"), n - 1)
                    pe.matmul(ps[:, n % 2, 0:384], XT[:, b, t * 128:t * 128 + 128], W("L1a.wqkv"),
                              start=True, stop=True).then_inc(sem("qkv1_ready"), 1)
                    if n >= 2:
                        turn(n - 2)
                turn(B * QT - 2)
                turn(B * QT - 1)

            def routing(stage, ne, router, turned):
                all_x(STAGE_FIRST[("ffn", stage)])
                for n in range(B * QT):
                    b, t = divmod(n, QT)
                    mm = pe.matmul(ps[:, 6, n * ne:n * ne + ne], XT[:, b, t * 128:t * 128 + 128], W(router),
                                   start=True, stop=True, skip_group_check=True)
                mm.then_inc(sem(turned), 1)

            def ranks():
                pe.wait_ge(sem("onehots"), 1)
                for n in range(B * QT):
                    o = ps[:, 7, n * 2 * NE:n * 2 * NE + 2 * NE]
                    pe.wait_ge(sem("onehot_sums"), n + 1)
                    pe.matmul(o, C("lower"), OHB[:, n, :], start=(n == 0), stop=False, skip_group_check=True)
                    mm = pe.matmul(o, C("ones"), OHS[:, n, :], start=False, stop=True, skip_group_check=True)
                mm.then_inc(sem("ranked"), 1)

            def experts(stage, ne):
                pre = f"e{stage}"
                units = ne * B

                def down(n):
                    e, b = divmod(n, B)
                    pe.wait_ge(sem(pre + "_hidden"), n + 1)
                    if n >= 2:
                        pe.wait_ge(sem(pre + "_added"), n - 1)
                    for t in range(QT):
                        mm = pe.matmul(ps[:, 4 + n % 2, t * 128:t * 128 + 128], HID[n % 2][:, t * 128:t * 128 + 128],
                                       EW[e % 2][:, 256:384], start=True, stop=True, skip_group_check=True)
                    mm.then_inc(sem(pre + "_down"), 1)

                for n in range(units):
                    e, b = divmod(n, B)
                    if b == 0:
                        pe.wait_ge(sem(f"{pre}_weights{e % 2}"), 16 * (e // 2 + 1))
                    if n >= 2:
                        pe.wait_ge(sem(pre + "_hidden"), n - 1)
                    pe.matmul(ps[:, n % 2, :], EW[e % 2][:, 0:128], XT[:, b, :], start=True, stop=True)\
                        .then_inc(sem(pre + "_gate"), 1)
                    pe.matmul(ps[:, 2 + n % 2, :], EW[e % 2][:, 128:256], XT[:, b, :], start=True, stop=True)\
                        .then_inc(sem(pre + "_up"), 1)
                    if n >= 1:
                        down(n - 1)
                down(units - 1)
                for b in range(B):
                    T = TAIL_OF[(f"ffn{stage}", b)]
                    pe.wait_ge(sem(pre + "_added"), units - B + b + 1)
                    bank = misc(T)
                    for t in range(QT):
                        mm = pe.transpose(bank[:, t * 128:t * 128 + 128], ACC[:, b, t, :], W("ident"))
                    mm.then_inc(sem("misc_filled"), 1)
                    ffn_tail(f"ffn{stage}", b)

            def ffn2():
                all_x(STAGE_FIRST[("ffn", 2)])
                pe.wait_ge(sem("wide_loaded"), 16)
                for b in range(B):
                    for c in range(FC):
                        i = b * FC + c
                        if i >= 2:
                            pe.wait_ge(sem("gated2"), i - 1)
                        pe.matmul(ps[:, i % 2, :], WWIDE("f2.w1", c * 128, 128), XT[:, b, :], start=True, stop=True)\
                            .then_inc(sem("w1_2"), 1)
                        pe.matmul(ps[:, 4 + i % 2, :], WWIDE("f2.w2", c * 128, 128), XT[:, b, :], start=True, stop=True)\
                            .then_inc(sem("w2_2"), 1)
                    for l, name, src in ((0, "f2.h1", G0), (1, "f2.h2", G1)):
                        pe.wait_ge(sem("gated2"), FC * (b + 1))
                        if l:
                            pe.wait_ge(sem("gelu2_done"), FC * (2 * b + 1))
                        for c in range(FC):
                            k = (2 * b + l) * FC + c
                            if k >= 2:
                                pe.wait_ge(sem("gelu2_done"), k - 1)
                            for i in range(FC):
                                mm = pe.matmul(ps[:, 2 + k % 2, :], WWIDE(name, i * 512 + c * 128, 128), src[:, i, :],
                                               start=(i == 0), stop=(i == FC - 1))
                            mm.then_inc(sem("hidden2"), 1)
                    T = TAIL_OF[("ffn2", b)]
                    bank = misc(T)
                    pe.wait_ge(sem("gelu2_done"), 2 * FC * (b + 1))
                    for i in range(FC):
                        mm = pe.matmul(bank, WWIDE("f2.w3", i * 128, 128), G0[:, i, :], start=(i == 0), stop=(i == FC - 1))
                    mm.then_inc(sem("misc_filled"), 1)
                    ffn_tail("ffn2", b)

            def self3():
                all_x(STAGE_FIRST[("self3", 0)])
                for b in range(B):
                    if b:
                        pe.wait_ge(sem("f3_copied"), 2 * b)
                    pe.matmul(ps[:, 0, :], W("L3a.w"), XT[:, b, :], start=True, stop=True).then_inc(sem("f3_ready"), 1)
                    for t in range(QT):
                        mm = pe.matmul(ps[:, 1, t * 128:t * 128 + 128], XT[:, b, t * 128:t * 128 + 128], W("L3a.w"),
                                       start=True, stop=True, skip_group_check=True)
                    mm.then_inc(sem("f3_ready"), 1)
                    pe.wait_ge(sem("f3_copied"), 2 * b + 2)
                    for t in range(QT):
                        n = b * QT + t
                        if n >= 2:
                            pe.wait_ge(sem("exp3_done"), n - 1)
                        bank = ps[:, 2 + n % 2, :]
                        pe.matmul(bank, FT3[:, t * 128:t * 128 + 128], FT3, start=True, stop=False)
                        lo, hi = max(0, t - 1), min(QT, t + 2)
                        for piece in range(3):
                            mm = pe.matmul(bank[:, lo * 128:hi * 128], C("ident"),
                                           C("band", piece * 384 + (lo - t + 1) * 128, (hi - lo) * 128),
                                           start=False, stop=(piece == 2))
                        mm.then_inc(sem("scores3"), 1)
                    for t in range(QT):
                        n = b * QT + t
                        pe.wait_ge(sem("probs3"), n + 1)
                        if n >= 2:
                            pe.wait_ge(sem("probs3_copied"), n - 1)
                        for kt in range(QT):
                            mm = pe.transpose(ps[:, 4 + n % 2, kt * 128:kt * 128 + 128], P3[:, t, kt * 128:kt * 128 + 128],
                                              W("ident"))
                        mm.then_inc(sem("probs3_turned"), 1)
                    T = TAIL_OF[("self30", b)]
                    bank = misc(T)
                    pe.wait_ge(sem("probs3_copied"), QT * (b + 1))
                    for kt in range(QT):
                        mm = pe.matmul(bank, FK3[:, kt, :], PT3[:, kt, :], start=(kt == 0), stop=(kt == QT - 1))
                    mm.then_inc(sem("misc_filled"), 1)
                    ffn_tail("self30", b)

            pe.wait_ge(sem("pack_loaded0"), 16)
            pe.wait_ge(sem("pack_loaded1"), 16)
            pe.wait_ge(sem("setup"), SETUP_DONE)
            pe.wait_ge(sem("x_loaded"), 16)
            for i, L in enumerate(LAYERS):
                bv = W(f"{L.name}.bv") if f"{L.name}.bv" in AT else W("zero")
                mm = pe.matmul(ps[:, MISC, i:i + 1], W(f"{L.name}.wo"), bv, start=True, stop=True)
            mm.then_inc(sem("bias_ready"), 1)
            pe.wait_ge(sem("bias_done"), 1)
            pe.wait_ge(sem("context_loaded"), 16)
            pe.wait_ge(sem("masks_ready"), 5)
            attention(0)
            ffn0()
            heads1()
            attention(1)
            routing(1, NE, "f1.router", "logits1")
            ranks()
            experts(1, NE)
            attention(2)
            ffn2()
            self3()
            attention(3)
            routing(3, NE3, "f3.router", "logits3")
            experts(3, NE3)
            for b in range(B):
                pe.wait_ge(sem("x_done"), len(TAILS) - B + b + 1)
                if b == 0:
                    pe.wait_ge(sem("x_done"), len(TAILS))
                for t in range(QT):
                    mm = pe.transpose(ps[:, b, t * 128:t * 128 + 128], XT[:, b, t * 128:t * 128 + 128], W("ident"))
                mm.then_inc(sem("result_turned"), 1)

        @block.vector
        def _(dve):
            links = [0]

            def link(ins):
                links[0] += 1
                ins.then_inc(sem("dve_link"), 1)
                dve.wait_ge(sem("dve_link"), links[0])

            filled, freed = sem("ring_filled"), sem("ring_freed")

            def front_operands(F):
                li, b = FRONTS[F]
                L = LAYERS[li]
                n = FILL_BASE[F]
                nk = KP if L.cross else S
                if L.rope:
                    dve.wait_ge(sem("tables_loaded"), 16 if li == 0 else 32)

                def bank(i):
                    dve.wait_ge(filled, n + i + 1)
                    return ps[:, RING + (n + i) % 2, :]

                def col(name):
                    return W(f"{L.name}.{name}") if f"{L.name}.{name}" in AT else W("zero")

                i = 0
                for X, what, width, tab in ((TQ, "q", S, 0), (TK, "k", nk, 2)):
                    if what == "k" and F:
                        dve.wait_ge(sem("keys_split"), F)
                    if L.rope:
                        ins = dve.scalar_tensor_tensor(out=X[:, 0:width], in0=bank(i), scalar=col("b" + what),
                                                       in1=tables[:, tab, :], op0=ALU.add, op1=ALU.mult)
                        ins.then_inc(freed, 1)
                        ins = dve.scalar_tensor_tensor(out=TR[:], in0=bank(i + 1), scalar=col(f"b{what}_rot"),
                                                       in1=tables[:, tab + 1, :], op0=ALU.add, op1=ALU.mult)
                        ins.then_inc(freed, 1)
                        dve.wait_ge(freed, n + i + 2)
                        ins = dve.tensor_tensor(X[:], X[:], TR[:], ALU.add)
                        if what == "q":
                            link(ins)
                        else:
                            ins.then_inc(sem("keys_ready"), 1)
                        i += 2
                    else:
                        dve.tensor_scalar(X[:, 0:width], bank(i)[:, 0:width], col("b" + what),
                                          L.scale if what == "q" else 1.0, ALU.add, ALU.mult).then_inc(freed, 1)
                        dve.wait_ge(freed, n + i + 1)
                        i += 1
                    if what == "q":
                        if F:
                            dve.wait_ge(sem("scratch_written"), 32 * F)
                        link(dve.tensor_copy(HQ[:, 0, :], TQ[:]))
                        link(dve.tensor_tensor(RQ[:], TQ[:], HQ[:, 0, :], ALU.subtract))
                        link(dve.tensor_copy(HQ[:, 1, :], RQ[:]))
                        dve.tensor_tensor(HQ[:, 2, :], RQ[:], HQ[:, 1, :], ALU.subtract).then_inc(sem("queries_split"), 1)
                    elif L.mask == "keys":
                        dve.tensor_tensor(TK[:, 0:nk], TK[:, 0:nk], MF[:, b, :], ALU.mult).then_inc(sem("keys_ready"), 1)
                if F >= 2:
                    dve.wait_ge(sem("values_done"), BLOCK_BASE[F - 1])
                par = F % 2
                v = bank(i)
                if L.cross:
                    dve.tensor_copy(VA[par][:, 0, :, 0:DH], v[:, 0:128].rearrange("p (h e) -> p h e", e=DH))
                    dve.tensor_copy(VA[par][:, 1, :, 0:DH], v[:, 128:256].rearrange("p (h e) -> p h e", e=DH))\
                        .then_inc(freed, 1)
                else:
                    for t in range(QT):
                        ins = dve.tensor_copy(VA[par][:, t, :, 0:DH],
                                              v[:, t * 128:t * 128 + 128].rearrange("p (h e) -> p h e", e=DH))
                    ins.then_inc(freed, 1)

            def max_unit(F, u):
                L = LAYERS[FRONTS[F][0]]
                n = FILL_BASE[F] + pre_fills(L) + u
                dve.wait_ge(filled, n + 1)
                bank = ps[:, RING + n % 2, :]
                i0, cnt = max_units(L)[u]
                if L.cross:
                    src = bank[:, 0:cnt * KP].rearrange("p (c k) -> p c k", k=KP)[:, :, 0:KC]
                else:
                    w = 128 * (i0 % QT + 1) if L.causal else S
                    src = bank[:, 0:w]
                dve.tensor_reduce(MX[:, i0:i0 + cnt], src, AX.X, ALU.max).then_inc(freed, 1)

            def split_maxima(F):
                dve.wait_ge(freed, FILL_BASE[F + 1] - 1)
                def piece(i):
                    return MP[:, :, i, :].rearrange("p t h -> p h t")
                m = MX[:].rearrange("p (h t) -> p h t", t=QT)
                r = MR[:].rearrange("p (h t) -> p h t", t=QT)
                link(dve.tensor_scalar(m, m, -1.0, None, ALU.mult))
                link(dve.tensor_copy(piece(0), m))
                link(dve.tensor_tensor(r, m, piece(0), ALU.subtract))
                link(dve.tensor_copy(piece(1), r))
                dve.tensor_tensor(piece(2), r, piece(1), ALU.subtract).then_inc(sem("maxima_split"), 1)

            def maxima_rows(F):
                n = FILL_BASE[F + 1] - 1
                dve.wait_ge(filled, n + 1)
                if F:
                    dve.wait_ge(sem("maxima_written"), 16 * F)
                dve.tensor_copy(MT[:], ps[:, RING + n % 2, :].bitcast(BF16)[0:48, 0:S]).then_inc(freed, 1)

            def misc_bank(n):
                dve.wait_ge(sem("misc_filled"), n + 1)
                return ps[:, MISC, :]

            def tail(T, stage, bias=None, scale=None):
                kind, F = TAILS[T]
                b = FRONTS[F][1] if kind == "attn" else F
                n = MISC_BASE[T] + (stage if kind == "attn" else stage - 5)
                if stage == 4:
                    return
                bank = misc_bank(n)
                if stage < 4:
                    o = bank.rearrange("p (t j r) -> p t j r", t=QT, j=4)
                    link(dve.reciprocal(RD[:].rearrange("p (t j) -> p t j", t=QT), o[:, :, :, DH:DH + 1].rearrange("p t j r -> p t (j r)")))
                    dst = OK[:, :, 32 * stage:32 * stage + 32].rearrange("p t (j e) -> p t j e", j=4)
                    r = RD[:].rearrange("p (t j) -> p t j", t=QT).unsqueeze(3).broadcast_to([128, QT, 4, DH])
                    dve.tensor_tensor(dst, o[:, :, :, 0:DH], r, ALU.mult).then_inc(sem("normalised"), 1)
                elif stage == 5:
                    if scale is not None:
                        dve.scalar_tensor_tensor(out=YT[:], in0=bank, scalar=scale, in1=XT[:, b, :],
                                                 op0=ALU.mult, op1=ALU.add).then_inc(sem("summed"), 1)
                    else:
                        dve.scalar_tensor_tensor(out=YT[:], in0=bank, scalar=bias, in1=XT[:, b, :],
                                                 op0=ALU.add, op1=ALU.add).then_inc(sem("summed"), 1)
                elif stage == 6:
                    dve.tensor_copy(YC[:], bank).then_inc(sem("centred"), 1)
                else:
                    dve.wait_ge(sem("rstd_ready"), T + 1)
                    dve.tensor_tensor(XT[:, b, :], YC[:], RS[:], ALU.mult).then_inc(sem("x_done"), 1)

            def attention(grp):
                front_operands(FRONTS.index((GROUPS[grp][0], 0)))
                for front, back, tl in steps(grp):
                    for p, fu, bu, phases in loop_of(front, back):
                        for u in fu:
                            max_unit(front, u)
                        if tl is not None and p in TAIL_AT:
                            tail(TAIL_OF[("attn", tl)], TAIL_AT[p], bias=BO[:, FRONTS[tl][0]:FRONTS[tl][0] + 1])
                        if "split" in phases:
                            split_maxima(front)
                        if "turn" in phases:
                            maxima_rows(front)
                        if "project" in phases and follows(front) is not None:
                            front_operands(front + 1)

            def ffn_tail(kind, b, **how):
                for stage in (5, 6, 7):
                    tail(TAIL_OF[(kind, b)], stage, **how)

            def scales(src, amax, scale, inv):
                link(dve.tensor_scalar(amax, amax, 1e-5, None, ALU.max))
                link(dve.reciprocal(scale, amax))
                dve.tensor_scalar(inv, amax, 1.0 / 127.0, None, ALU.mult)
                link(dve.tensor_scalar(scale, scale, 127.0, None, ALU.mult))

            def ffn0():
                dve.wait_ge(sem("x_done"), STAGE_FIRST[("ffn", 0)])
                for i, (w, wq) in enumerate((("f0.w1", WQ1), ("f0.w2", WQ2))):
                    dve.tensor_reduce(W0S[:, i:i + 1], W(w), AX.X, ALU.add, apply_absolute_value=True)\
                        .then_inc(sem("w0_sums"), 1)
                dve.wait_ge(sem("w0_means"), 1)
                link(dve.tensor_scalar(W0M, ps[:, 6, 0:2], 1.0 / 512.0, 1e-5, ALU.mult, ALU.max))
                link(dve.reciprocal(W0R, W0M))
                for i, (w, wq) in enumerate((("f0.w1", WQ1), ("f0.w2", WQ2))):
                    link(dve.tensor_scalar(wq, W(w), W0R[:, i:i + 1], MAGIC, ALU.mult, ALU.add))
                    link(dve.tensor_scalar(wq, wq, MAGIC, 1.0, ALU.subtract, ALU.min))
                    dve.tensor_scalar(wq, wq, -1.0, W0M[:, i:i + 1], ALU.max, ALU.mult).then_inc(sem("w0_ready"), 1)
                dve.wait_ge(sem("w0_ready"), 2)
                for b in range(B):
                    dve.wait_ge(sem("x0_turned"), b + 1)
                    if b:
                        dve.wait_ge(sem("x0_back"), b)
                    x = ps[:, 0, :].rearrange("p (t d) -> p t d", t=QT)
                    link(dve.tensor_reduce(AM[:, 0:QT], x, AX.X, ALU.max, apply_absolute_value=True))
                    scales(None, AM[:, 0:QT], SC[:, 0:QT], IV[:, 0:QT])
                    for t in range(QT):
                        ins = dve.tensor_scalar(XQ[:, t, :], x[:, t, :], SC[:, t:t + 1], MAGIC, ALU.mult, ALU.add)
                    link(ins)
                    for t in range(QT):
                        ins = dve.tensor_scalar(XQ[:, t, :], XQ[:, t, :], MAGIC, IV[:, t:t + 1], ALU.subtract, ALU.mult)
                    ins.then_inc(sem("q0_rounded"), 1)
                    for c in range(FC):
                        dve.wait_ge(sem("conv0_centre"), b * FC + c + 1)
                        h = ps[:, 2 + c, :]
                        link(dve.scalar_tensor_tensor(out=HC[:, c, 1:S], in0=h[:, 0:S - 1], scalar=W("f0.taps", 3 * c, 1),
                                                      in1=HC[:, c, 1:S], op0=ALU.mult, op1=ALU.add))
                        dve.scalar_tensor_tensor(out=HC[:, c, 0:S - 1], in0=h[:, 1:S], scalar=W("f0.taps", 3 * c + 2, 1),
                                                 in1=HC[:, c, 0:S - 1], op0=ALU.mult, op1=ALU.add)\
                            .then_inc(sem("conv_done"), 1)
                    for t in range(QT):
                        n = b * QT + t
                        dve.wait_ge(sem("h0_turned"), n + 1)
                        if n:
                            dve.wait_ge(sem("h0_back"), n)
                        link(dve.tensor_reduce(AM[:, 4:5], ps[:, 0, :], AX.X, ALU.max, apply_absolute_value=True))
                        scales(None, AM[:, 4:5], SC[:, 4:5], IV[:, 4:5])
                        link(dve.tensor_scalar(HR, ps[:, 0, :], SC[:, 4:5], MAGIC, ALU.mult, ALU.add))
                        dve.tensor_scalar(HR, HR, MAGIC, IV[:, 4:5], ALU.subtract, ALU.mult)\
                            .then_inc(sem("h0_rounded"), 1)
                    ffn_tail("ffn0", b, bias=W("zero"))

            def heads1():
                dve.wait_ge(sem("x_done"), STAGE_FIRST[("heads", 1)])

                def scores(n):
                    i = n % 2
                    q, k = QKV1[i][:, 0], QKV1[i][:, 1]
                    p = PR1[i].rearrange("p (h g e) -> p h g e", h=H, g=H)
                    dve.wait_ge(sem("qkv1_copied"), n + 1)
                    link(dve.tensor_tensor(p, q.unsqueeze(2).broadcast_to([128, H, H, DH]),
                                           k.unsqueeze(1).broadcast_to([128, H, H, DH]), ALU.mult))
                    if n >= 2:
                        dve.wait_ge(sem("values1_weighted"), n - 1)
                    link(dve.tensor_reduce(SC1[i], p, AX.X, ALU.add))
                    link(dve.tensor_reduce(MH1[i], SC1[i], AX.X, ALU.max))
                    dve.tensor_tensor(SC1[i], SC1[i], MH1[i].unsqueeze(2).broadcast_to([128, H, H]), ALU.subtract)\
                        .then_inc(sem("scores1_shifted"), 1)

                def mix(n):
                    i = n % 2
                    dve.wait_ge(sem("exp1h_done"), n + 1)
                    link(dve.tensor_reduce(RH1[i], SC1[i], AX.X, ALU.add))
                    link(dve.reciprocal(RH1[i], RH1[i]))
                    if n >= 2:
                        dve.wait_ge(sem("mixed1_turned"), n - 1)
                    dve.wait_ge(sem("values1_weighted"), n + 1)
                    link(dve.tensor_reduce(OH1[i], PV1[i].rearrange("p (h e g) -> p h e g", h=H, g=H), AX.X, ALU.add))
                    dve.tensor_tensor(OH1[i], OH1[i], RH1[i].unsqueeze(2).broadcast_to([128, H, DH]), ALU.mult)\
                        .then_inc(sem("heads1_mixed"), 1)
                    if n % QT == QT - 1:
                        ffn_tail("heads1", n // QT, bias=W("L1a.bo"))

                for n in range(B * QT):
                    scores(n)
                    if n >= 1:
                        mix(n - 1)
                mix(B * QT - 1)

            def routing1():
                dve.wait_ge(sem("logits1"), 1)
                lg = ps[:, 6, 0:B * QT * NE].rearrange("p (n e) -> p n e", e=NE)
                link(dve.tensor_reduce(RM[:], lg, AX.X, ALU.max))
                dve.tensor_tensor(E16, lg, RM[:].unsqueeze(2).broadcast_to([128, 16, NE]), ALU.subtract)\
                    .then_inc(sem("logits1_shifted"), 1)
                dve.wait_ge(sem("exp1_done"), 1)
                link(dve.tensor_reduce(RM[:], E16, AX.X, ALU.add))
                link(dve.reciprocal(RM[:], RM[:]))
                link(dve.tensor_tensor(E16, E16, RM[:].unsqueeze(2).broadcast_to([128, 16, NE]), ALU.mult))
                for n in range(B * QT):
                    link(dve.max(T8[:, n, :], E16[:, n, :]))
                    ins = dve.max_index(I8[:, n, :], T8[:, n, :], E16[:, n, :])
                link(ins)
                link(dve.tensor_copy(I8F, I8[:]))
                iota = W("iota").unsqueeze(1).broadcast_to([128, 16, NE])
                for k in range(2):
                    ins = dve.tensor_tensor(OHF[:, :, k, :], iota, I8F[:, :, k:k + 1].broadcast_to([128, 16, NE]),
                                            ALU.is_equal)
                link(ins)
                dve.tensor_copy(OHB, OHF.rearrange("p n k e -> p n (k e)")).then_inc(sem("onehots"), 1)
                dve.memset(OHS[:, 0, :], 0.0).then_inc(sem("onehot_sums"), 1)
                dve.wait_ge(sem("onehots"), 1)
                for n in range(1, B * QT):
                    dve.wait_ge(sem("onehot_sums"), n)
                    dve.tensor_tensor(OHS[:, n, :], OHS[:, n - 1, :], OHB[:, n - 1, :], ALU.add)\
                        .then_inc(sem("onehot_sums"), 1)
                dve.wait_ge(sem("ranked"), 1)
                ohf = OHF.rearrange("p n k e -> p (n k e)")
                link(dve.scalar_tensor_tensor(out=ohf, in0=ps[:, 7, :], scalar=float(CAP), in1=ohf,
                                              op0=ALU.is_lt, op1=ALU.mult))
                link(dve.tensor_tensor(WC, OHF[:, :, 0, :], T8[:, :, 0:1].broadcast_to([128, 16, NE]), ALU.mult))
                link(dve.tensor_tensor(E16, OHF[:, :, 1, :], T8[:, :, 1:2].broadcast_to([128, 16, NE]), ALU.mult))
                link(dve.tensor_tensor(WC, WC, E16, ALU.add))

            def routing3():
                dve.wait_ge(sem("logits3"), 1)
                lg = ps[:, 6, 0:B * QT * NE3].rearrange("p (n e) -> p n e", e=NE3)
                w = WC[:, :, 0:NE3]
                inh, fb, fm, t = (R3[i] for i in range(4))
                link(dve.reciprocal(RM[:, 0:1], W("f3.temperature")))
                dve.tensor_scalar(inh, lg, RM[:, 0:1], None, ALU.mult).then_inc(sem("logits3_scaled"), 1)
                dve.wait_ge(sem("exp3r_done"), 1)
                link(dve.tensor_scalar(inh, inh, 1.0, None, ALU.add))
                link(dve.reciprocal(inh, inh))
                link(dve.tensor_scalar(t, inh, float(GOLD), None, ALU.subtract))
                link(dve.scalar_tensor_tensor(out=fb, in0=t, scalar=-1.0, in1=t, op0=ALU.mult, op1=ALU.max))
                dve.tensor_copy(t, fb).then_inc(sem("dist3_ready"), 1)
                dve.wait_ge(sem("exp3r_done"), 3)
                link(dve.tensor_scalar(w, inh, GOLD_LOW, None, ALU.is_ge))
                link(dve.scalar_tensor_tensor(out=w, in0=inh, scalar=GOLD_HIGH, in1=w, op0=ALU.is_le, op1=ALU.mult))
                link(dve.tensor_tensor(w, w, t, ALU.mult))
                for n in range(B * QT):
                    link(dve.max(T8[:, n, :], fb[:, n, :]))
                    ins = dve.max_index(I8[:, n, :], T8[:, n, :], fb[:, n, :])
                link(ins)
                link(dve.tensor_copy(I8F, I8[:]))
                iota = W("iota", 0, NE3).unsqueeze(1).broadcast_to([128, 16, NE3])
                link(dve.tensor_tensor(fm, iota, I8F[:, :, 0:1].broadcast_to([128, 16, NE3]), ALU.is_equal))
                link(dve.tensor_tensor(t, iota, I8F[:, :, 1:2].broadcast_to([128, 16, NE3]), ALU.is_equal))
                link(dve.tensor_tensor(fm, fm, t, ALU.add))
                link(dve.tensor_tensor(fm, fm, fb, ALU.mult))

                def normalise(x):
                    link(dve.tensor_reduce(RM[:], x, AX.X, ALU.add))
                    link(dve.tensor_scalar(RM[:], RM[:], 1e-8, None, ALU.max))
                    link(dve.reciprocal(RM[:], RM[:]))
                    link(dve.tensor_tensor(x, x, RM[:].unsqueeze(2).broadcast_to([128, 16, NE3]), ALU.mult))
                normalise(fm)
                link(dve.tensor_reduce(RM[:], w, AX.X, ALU.add))
                link(dve.tensor_scalar(RM[:], RM[:], 1e-8, None, ALU.is_lt))
                link(dve.tensor_tensor(fm, fm, RM[:].unsqueeze(2).broadcast_to([128, 16, NE3]), ALU.mult))
                link(dve.tensor_scalar(RM[:], RM[:], -1.0, 1.0, ALU.mult, ALU.add))
                link(dve.tensor_tensor(w, w, RM[:].unsqueeze(2).broadcast_to([128, 16, NE3]), ALU.mult))
                link(dve.tensor_tensor(w, w, fm, ALU.add))
                normalise(w)

            def experts(stage, ne):
                pre = f"e{stage}"
                units = ne * B

                def add(n):
                    e, b = divmod(n, B)
                    dve.wait_ge(sem(pre + "_down"), n + 1)
                    if e:
                        dve.wait_ge(sem(pre + "_added"), n - B + 1)
                    for t in range(QT):
                        o, p = ACC[:, b, t, :], ps[:, 4 + n % 2, t * 128:t * 128 + 128]
                        s = WC[:, b * QT + t, e:e + 1]
                        if e == 0:
                            ins = dve.tensor_scalar(o, p, s, None, ALU.mult)
                        else:
                            ins = dve.scalar_tensor_tensor(out=o, in0=p, scalar=s, in1=o, op0=ALU.mult, op1=ALU.add)
                    ins.then_inc(sem(pre + "_added"), 1)

                for n in range(units):
                    dve.wait_ge(sem(pre + "_silu"), n + 1)
                    dve.wait_ge(sem(pre + "_up"), n + 1)
                    if n >= 2:
                        dve.wait_ge(sem(pre + "_down"), n - 1)
                    dve.tensor_tensor(HID[n % 2], SG[n % 2], ps[:, 2 + n % 2, :], ALU.mult)\
                        .then_inc(sem(pre + "_hidden"), 1)
                    if n >= 1:
                        add(n - 1)
                add(units - 1)
                for b in range(B):
                    ffn_tail(f"ffn{stage}", b, bias=W("zero"))

            def ffn2():
                for b in range(B):
                    for c in range(FC):
                        i = b * FC + c
                        dve.wait_ge(sem("silu2_done"), i + 1)
                        dve.wait_ge(sem("w2_2"), i + 1)
                        dve.scalar_tensor_tensor(out=G0[:, c, :], in0=ps[:, 4 + i % 2, :], scalar=W("f2.s2", c, 1),
                                                 in1=SG2[i % 2], op0=ALU.mult, op1=ALU.mult).then_inc(sem("gated2"), 1)
                    ffn_tail("ffn2", b, scale=W("f2.s3"))

            def self3():
                for b in range(B):
                    dve.wait_ge(sem("f3_ready"), 2 * b + 1)
                    if b:
                        dve.wait_ge(sem("scores3"), QT * b)
                        dve.wait_ge(sem("misc_filled"), MISC_BASE[TAIL_OF[("self30", b - 1)]] + 1)
                    dve.tensor_scalar(FT3, ps[:, 0, :], W("L3a.b"), None, ALU.add).then_inc(sem("f3_copied"), 1)
                    dve.wait_ge(sem("f3_ready"), 2 * b + 2)
                    dve.tensor_copy(FK3.rearrange("p t d -> p (t d)"), ps[:, 1, :]).then_inc(sem("f3_copied"), 1)
                    for t in range(QT):
                        n = b * QT + t
                        dve.wait_ge(sem("scores3"), n + 1)
                        dve.tensor_reduce(M3[:, n:n + 1], ps[:, 2 + n % 2, :], AX.X, ALU.max, negate=True)\
                            .then_inc(sem("max3"), 1)
                    for t in range(QT):
                        n = b * QT + t
                        dve.wait_ge(sem("exp3_done"), n + 1)
                        link(dve.reciprocal(L3R[:, n:n + 1], L3S[:, n:n + 1]))
                        dve.tensor_scalar(P3[:, t, :], P3[:, t, :], L3R[:, n:n + 1], None, ALU.mult)\
                            .then_inc(sem("probs3"), 1)
                    ffn_tail("self30", b, bias=W("L3a.b"))

            dve.wait_ge(sem("const_loaded"), 16)
            dve.tensor_copy(const[:], WORK[:, 0:NCONST]).then_inc(sem("setup"), 1)
            for i in range(2):
                dve.memset(VA[i][:], 0.0).then_inc(sem("setup"), 1)
                dve.memset(QH[i][:], 0.0).then_inc(sem("setup"), 1)
            dve.wait_ge(sem("setup"), SETUP_DONE)
            for i in range(2):
                dve.memset(VA[i][:, :, :, DH:DH + 1], 1.0).then_inc(sem("masks_ready"), 1)
            dve.wait_ge(sem("bias_ready"), 1)
            dve.wait_ge(sem("pack_loaded1"), 16)
            for i, L in enumerate(LAYERS):
                ins = dve.tensor_tensor(BO[:, i:i + 1], ps[:, MISC, i:i + 1], W(f"{L.name}.bo") if f"{L.name}.bo" in AT else W("zero"),
                                        ALU.add)
            ins.then_inc(sem("bias_done"), 1)
            dve.wait_ge(sem("bias_done"), 1)
            dve.wait_ge(sem("mask_loaded"), 16 * 3)
            big = 1e20 / 8 ** 0.5
            dve.tensor_scalar(MQ2[:].rearrange("p t k -> p (t k)"), MU[:], 1.0, big, ALU.subtract, ALU.mult)\
                .then_inc(sem("masks_ready"), 1)
            dve.tensor_scalar(MT2[:], MU2[:], 1.0, big, ALU.subtract, ALU.mult).then_inc(sem("masks_ready"), 1)
            dve.memset(MR2[:], 0.0).then_inc(sem("mr2_clear"), 1)
            dve.wait_ge(sem("mr2_clear"), 1)
            dve.tensor_scalar(MR2[0:32, :], MU3[0:32, :], 1.0, big, ALU.subtract, ALU.mult).then_inc(sem("masks_ready"), 1)
            dve.wait_ge(sem("mask_keys_loaded"), 16)
            dve.tensor_copy(MF[:].rearrange("p b k -> p (b k)"), MU4[:]).then_inc(sem("mask_keys"), 1)
            dve.wait_ge(sem("setup"), SETUP_DONE)
            attention(0)
            ffn0()
            heads1()
            attention(1)
            routing1()
            experts(1, NE)
            attention(2)
            ffn2()
            self3()
            attention(3)
            routing3()
            experts(3, NE3)
            for b in range(B):
                dve.wait_ge(sem("result_turned"), b + 1)
                dve.tensor_copy(OUT[:, b, :, :].rearrange("p t d -> p (t d)"), ps[:, b, :]).then_inc(sem("result_ready"), 1)

        @block.scalar
        def _(act):
            links = [0]

            def link(ins):
                links[0] += 1
                ins.then_inc(sem("act_link"), 1)
                act.wait_ge(sem("act_link"), links[0])

            def exp_pair(F, n):
                L = LAYERS[FRONTS[F][0]]
                N = PAIR_BASE[F] + n
                act.wait_ge(sem("scores_ready"), N + 1)
                if N >= NSLOT:
                    act.wait_ge(sem("values_done"), LAST_READER[N - NSLOT] + 1)
                u = pair_units(L)[n]
                q0 = 128 * u[2] if L.causal else 0
                bank = EXPB + 2 * (N % 2)
                act.activation(PB[:, N % NSLOT, :, q0:S], ps[:, bank:bank + 2, q0:S], ACT.Exp).then_inc(sem("exp_done"), 1)

            def copy_outputs(F, g):
                L = LAYERS[FRONTS[F][0]]
                k = [i for i, blk in enumerate(value_blocks(L)) if blk[1] == g][-1]
                act.wait_ge(sem("values_done"), BLOCK_BASE[F] + k + 1)
                if F:
                    T = TAIL_OF[("attn", F - 1)]
                    act.wait_ge(sem("misc_filled"), MISC_BASE[T] + g + 1)
                act.activation(US[:, g, :], ps[:, UB, :], ACT.Copy).then_inc(sem("outputs_copied"), 1)

            def tail(T, stage):
                kind, F = TAILS[T]
                n = MISC_BASE[T + 1] - 1
                if stage == 4:
                    act.wait_ge(sem("misc_filled"), MISC_BASE[T] + 5)
                    act.activation(OT[:], ps[:, MISC, :], ACT.Copy).then_inc(sem("outputs_turned"), 1)
                elif stage == 6:
                    act.wait_ge(sem("centred"), T + 1)
                    act.activation(SQ[:], YC[:], ACT.Square).then_inc(sem("squared"), 1)
                elif stage == 7:
                    act.wait_ge(sem("misc_filled"), n + 1)
                    act.activation(LV[:], ps[:, MISC, :], ACT.Ln, bias=W("eps")).then_inc(sem("log_ready"), 1)
                    act.wait_ge(sem("log_ready"), T + 1)
                    act.activation(RS[:], LV[:], ACT.Exp, scale=-0.5).then_inc(sem("rstd_ready"), 1)

            def attention(grp):
                for front, back, tl in steps(grp):
                    L = LAYERS[FRONTS[back][0]] if back is not None else None
                    ends = {}
                    if L is not None:
                        for blk in value_blocks(L):
                            ends[blk[1]] = blk[0]
                    g = 0
                    for p, fu, bu, phases in loop_of(front, back):
                        for u in bu:
                            exp_pair(back, u)
                            while g < 4 and ends[g] + 3 <= u:
                                copy_outputs(back, g)
                                g += 1
                        if tl is not None and p in TAIL_AT:
                            tail(TAIL_OF[("attn", tl)], TAIL_AT[p])
                    while L is not None and g < 4:
                        copy_outputs(back, g)
                        g += 1

            def log_exp_tables():
                act.preload_act_table_set("natural_log_exp_and_others")

            def ffn_tail(kind, b):
                log_exp_tables()
                tail(TAIL_OF[(kind, b)], 6)
                tail(TAIL_OF[(kind, b)], 7)

            def ffn0():
                act.wait_ge(sem("x_done"), STAGE_FIRST[("ffn", 0)])
                for b in range(B):
                    act.wait_ge(sem("x0_back"), b + 1)
                    if b:
                        act.wait_ge(sem("h0_ready"), FC * b)
                    act.activation(XQT, ps[:, 1, :], ACT.Copy).then_inc(sem("q0_turned"), 1)
                    for c in range(FC):
                        act.wait_ge(sem("h0_ready"), b * FC + c + 1)
                        if b:
                            act.wait_ge(sem("silu0_done"), FC * (b - 1) + c + 1)
                        act.activation(HC[:, c, :], ps[:, 2 + c, :], ACT.Identity, bias=W("f0.bias", c, 1),
                                       scale=W("f0.taps", 3 * c + 1, 1)).then_inc(sem("conv0_centre"), 1)
                    if b:
                        act.wait_ge(sem("h0_turned"), QT * b)
                    for c in range(FC):
                        act.wait_ge(sem("conv_done"), b * FC + c + 1)
                        act.activation(HS[:, c, :], HC[:, c, :], ACT.Silu).then_inc(sem("silu0_done"), 1)
                    if b:
                        act.wait_ge(sem("misc_filled"), MISC_BASE[TAIL_OF[("ffn0", b - 1)]] + 1)
                    for t in range(QT):
                        act.wait_ge(sem("h0_back"), b * QT + t + 1)
                        act.activation(HQT[:, :, t * 128:t * 128 + 128], ps[:, 1, :].rearrange("p (c s) -> p c s", c=FC),
                                       ACT.Copy).then_inc(sem("h0_back_copied"), 1)
                    ffn_tail("ffn0", b)

            def heads1():
                act.wait_ge(sem("x_done"), STAGE_FIRST[("heads", 1)])

                def weigh(n):
                    act.wait_ge(sem("scores1_shifted"), n + 1)
                    act.activation(SC1[n % 2], SC1[n % 2], ACT.Exp, scale=1 / 8.0).then_inc(sem("exp1h_done"), 1)

                def finish(b):
                    act.wait_ge(sem("mixed1_turned"), QT * (b + 1))
                    if b:
                        act.wait_ge(sem("misc_filled"), MISC_BASE[TAIL_OF[("heads1", b - 1)]] + 1)
                    act.activation(OT1, ps[:, 2 + b % 2, :], ACT.Copy).then_inc(sem("mixed1_copied"), 1)
                    ffn_tail("heads1", b)

                for n in range(B * QT):
                    act.wait_ge(sem("qkv1_ready"), n + 1)
                    if n >= 2:
                        act.wait_ge(sem("values1_weighted"), n - 1)
                    act.activation(QKV1[n % 2].rearrange("p w h e -> p (w h e)"), ps[:, n % 2, 0:384], ACT.Copy)\
                        .then_inc(sem("qkv1_copied"), 1)
                    if n and n % QT == 1 and n > QT:
                        finish(n // QT - 1)
                    if n >= 1:
                        weigh(n - 1)
                weigh(B * QT - 1)
                finish(B - 1)

            def experts(stage, ne):
                pre = f"e{stage}"
                for n in range(ne * B):
                    act.wait_ge(sem(pre + "_gate"), n + 1)
                    if n >= 2:
                        act.wait_ge(sem(pre + "_hidden"), n - 1)
                    act.activation(SG[n % 2], ps[:, n % 2, :], ACT.Silu).then_inc(sem(pre + "_silu"), 1)
                for b in range(B):
                    ffn_tail(f"ffn{stage}", b)

            def ffn2():
                for b in range(B):
                    for c in range(FC):
                        i = b * FC + c
                        act.wait_ge(sem("w1_2"), i + 1)
                        if i >= 2:
                            act.wait_ge(sem("gated2"), i - 1)
                        act.activation(SG2[i % 2], ps[:, i % 2, :], ACT.Silu, scale=W("f2.s1", c, 1)).then_inc(sem("silu2_done"), 1)
                    for l, dst, s in ((0, G1, "f2.sh1"), (1, G0, "f2.sh2")):
                        for c in range(FC):
                            k = (2 * b + l) * FC + c
                            act.wait_ge(sem("hidden2"), k + 1)
                            if b and l == 0:
                                act.wait_ge(sem("hidden2"), 2 * FC * b)
                            if b and l == 1:
                                act.wait_ge(sem("misc_filled"), MISC_BASE[TAIL_OF[("ffn2", b - 1)]] + 1)
                            act.activation(dst[:, c, :], ps[:, 2 + k % 2, :], ACT.Gelu, scale=W(s, c, 1))\
                                .then_inc(sem("gelu2_done"), 1)
                    ffn_tail("ffn2", b)

            def self3():
                for b in range(B):
                    for t in range(QT):
                        n = b * QT + t
                        act.wait_ge(sem("max3"), n + 1)
                        if b:
                            act.wait_ge(sem("probs3_turned"), n - QT + 1)
                        act.activation(P3[:, t, :], ps[:, 2 + n % 2, :], ACT.Exp, bias=M3[:, n:n + 1],
                                       accum_out=L3S[:, n:n + 1]).then_inc(sem("exp3_done"), 1)
                    if b:
                        act.wait_ge(sem("misc_filled"), MISC_BASE[TAIL_OF[("self30", b - 1)]] + 1)
                    for t in range(QT):
                        n = b * QT + t
                        act.wait_ge(sem("probs3_turned"), n + 1)
                        act.activation(PT3[:, :, t * 128:t * 128 + 128],
                                       ps[:, 4 + n % 2, :].rearrange("p (k s) -> p k s", k=QT), ACT.Copy)\
                            .then_inc(sem("probs3_copied"), 1)
                    ffn_tail("self30", b)

            act.wait_ge(sem("pack_loaded0"), 16)
            act.wait_ge(sem("pack_loaded1"), 16)
            act.wait_ge(sem("setup"), SETUP_DONE)
            log_exp_tables()
            attention(0)
            ffn0()
            heads1()
            attention(1)
            act.wait_ge(sem("logits1_shifted"), 1)
            act.activation(E16, E16, ACT.Exp).then_inc(sem("exp1_done"), 1)
            experts(1, NE)
            attention(2)
            ffn2()
            self3()
            attention(3)
            act.wait_ge(sem("logits3_scaled"), 1)
            act.activation(R3[0], R3[0], ACT.Exp, scale=-1.0).then_inc(sem("exp3r_done"), 1)
            act.wait_ge(sem("dist3_ready"), 1)
            act.activation(R3[3], R3[3], ACT.Exp, scale=-1.0 / 0.1).then_inc(sem("exp3r_done"), 1)
            act.activation(R3[1], R3[1], ACT.Exp, scale=-1.0 / 0.3).then_inc(sem("exp3r_done"), 1)
            experts(3, NE3)

        @block.gpsimd
        def _(pool):
            links = [0]

            def link(ins):
                links[0] += 1
                ins.then_inc(sem("pool_link"), 1)
                pool.wait_ge(sem("pool_link"), links[0])

            for i in range(2):
                pool.memset(KH[i][:], 0.0).then_inc(sem("setup"), 1)
            pool.memset(HK[:], 0.0).then_inc(sem("setup"), 1)
            pool.wait_ge(sem("setup"), SETUP_DONE)
            for i in range(2):
                pool.memset(QH[i][32:64, :, :], 1.0).then_inc(sem("ones_rows"), 1)
            pool.wait_ge(sem("ones_rows"), 2)
            made = [0]

            def split_keys(F):
                li, b = FRONTS[F]
                L = LAYERS[li]
                nk = KP if L.cross else S
                if L.rope or L.mask == "keys":
                    made[0] += 1
                    pool.wait_ge(sem("keys_ready"), made[0])
                else:
                    pool.wait_ge(sem("ring_freed"), FILL_BASE[F] + 2)
                if F:
                    pool.wait_ge(sem("scratch_written"), 32 * F)
                link(pool.tensor_copy(HK[:, 0, 0:nk], TK[:, 0:nk]))
                link(pool.tensor_tensor(RK[:, 0:nk], TK[:, 0:nk], HK[:, 0, 0:nk], ALU.subtract))
                link(pool.tensor_copy(HK[:, 1, 0:nk], RK[:, 0:nk]))
                pool.tensor_tensor(HK[:, 2, 0:nk], RK[:, 0:nk], HK[:, 1, 0:nk], ALU.subtract).then_inc(sem("keys_split"), 1)
                if L.mask == "keys":
                    pool.wait_ge(sem("keys_split"), F + 1)
                    pool.wait_ge(sem("mask_keys"), 1)
                    pool.wait_ge(sem("mconst_loaded"), 16)
                    if b:
                        pool.wait_ge(sem("operands_loaded"), 16 * OPERAND_DMAS[F])
                    link(pool.tensor_scalar(MKF[:], MF[0:3, b, :], 1.0, mconst[:], ALU.subtract, ALU.mult))
                    pool.tensor_copy(MK[:], MKF[:].unsqueeze(1).broadcast_to([3, H, KP])).then_inc(sem("mask_rows"), 1)
                    pool.wait_ge(sem("mask_rows"), b + 1)

            def attention(grp):
                for front, back, tl in steps(grp):
                    if front is not None:
                        split_keys(front)

            def heads1():
                pool.wait_ge(sem("x_done"), STAGE_FIRST[("heads", 1)])
                for n in range(B * QT):
                    i = n % 2
                    pool.wait_ge(sem("exp1h_done"), n + 1)
                    if n >= 2:
                        pool.wait_ge(sem("heads1_mixed"), n - 1)
                    v = QKV1[i][:, 2].rearrange("p g e -> p e g").unsqueeze(1).broadcast_to([128, H, DH, H])
                    pool.tensor_tensor(PV1[i].rearrange("p (h e g) -> p h e g", h=H, g=H),
                                       SC1[i].unsqueeze(2).broadcast_to([128, H, DH, H]), v, ALU.mult)\
                        .then_inc(sem("values1_weighted"), 1)

            attention(0)
            heads1()
            attention(1)
            attention(2)
            attention(3)

        @block.sync
        def _(sp):
            split = AT["split"][0]
            sp.dma_start(XT[:], d["xT"]).then_inc(sem("x_loaded"), 16)
            sp.dma_start(pack[:, 0:split], d["pack"][:, 0:split]).then_inc(sem("pack_loaded0"), 16)
            sp.dma_start(WORK[:, 0:NCONST], d["const"]).then_inc(sem("const_loaded"), 16)
            sp.dma_start(tables[:], d["tables"][:, 0:4, :]).then_inc(sem("tables_loaded"), 16)
            sp.dma_start(pack[:, split:NPACK], d["pack"][:, split:NPACK]).then_inc(sem("pack_loaded1"), 16)
            sp.dma_start(CT[:], d["cT"]).then_inc(sem("context_loaded"), 16)
            sp.dma_start(MU[:], d["mask_q"]).then_inc(sem("mask_loaded"), 16)
            sp.dma_start(MU2[:], d["mask_k"][0:128, :]).then_inc(sem("mask_loaded"), 16)
            sp.dma_start(MU3[0:32, :], d["mask_k"][128:160, :]).then_inc(sem("mask_loaded"), 16)
            sp.dma_start(mconst[:], d["mconst"]).then_inc(sem("mconst_loaded"), 16)
            sp.dma_start(MU4[:], d["mask_c"][0:1, :].broadcast_to([128, B * KP])).then_inc(sem("mask_keys_loaded"), 16)
            sp.wait_ge(sem("ones_rows"), 2)
            sp.wait_ge(sem("setup"), SETUP_DONE)
            for i in range(2):
                sp.dma_start(KH[i][ROW_M:ROW_M + 3, :, :], QH[i][ROW_MASK:ROW_MASK + 3, :, :]).then_inc(sem("key_ones"), 16)

            def load_operands(F):
                li, b = FRONTS[F]
                L = LAYERS[li]
                par = F % 2
                nk = KP if L.cross else S
                if F >= 2:
                    sp.wait_ge(sem("operands_loaded"), 16 * OPERAND_DMAS[F - 1])
                sp.wait_ge(sem("queries_split"), F + 1)
                sp.dma_start(scratch[par, 0].rearrange("a p s -> p a s"), HQ[:]).then_inc(sem("scratch_written"), 16)
                sp.wait_ge(sem("keys_split"), F + 1)
                sp.dma_start(scratch[par, 1].rearrange("a p s -> p a s")[:, :, 0:nk], HK[:, :, 0:nk])\
                    .then_inc(sem("scratch_written"), 16)
                if F >= 2:
                    sp.wait_ge(sem("values_done"), BLOCK_BASE[F - 1])
                else:
                    sp.wait_ge(sem("key_ones"), 32)
                sp.dma_start(QH[par][ROW_M:ROW_M + 3, :, :], d["zrow"]).then_inc(sem("operands_loaded"), 16)
                sp.wait_ge(sem("scratch_written"), 32 * (F + 1))
                for which, dst, width, plan in ((0, QH, S, PIECES_Q), (1, KH, nk, PIECES_K)):
                    for slot, cnt, first, same in plan:
                        for i in range(cnt):
                            piece = first if same else first + i
                            r = DH * (slot + i)
                            sp.dma_start(dst[par][r:r + DH, :, 0:width],
                                         scratch[par, which, piece].rearrange("(h e) s -> e h s", e=DH)[:, :, 0:width])\
                                .then_inc(sem("operands_loaded"), 16)
                if L.mask == "keys":
                    sp.wait_ge(sem("mask_rows"), b + 1)
                    sp.dma_start(KH[par][ROW_MASK:ROW_MASK + 3, :, 0:KP], MK[:]).then_inc(sem("operands_loaded"), 16)
                elif L.name == "L2a" and b < 2:
                    sp.dma_start(KH[par][ROW_MASK:ROW_MASK + 3, :, :], d["zrow"]).then_inc(sem("operands_loaded"), 16)

            def load_maxima(F):
                sp.wait_ge(sem("ring_freed"), FILL_BASE[F + 1])
                par = F % 2
                if F >= 2:
                    sp.wait_ge(sem("maxima_loaded"), 16 * (F - 1))
                sp.dma_start(mscratch[par], MT[:]).then_inc(sem("maxima_written"), 16)
                sp.wait_ge(sem("maxima_written"), 16 * (F + 1))
                sp.dma_start(QH[par][ROW_M:ROW_M + 3, :, :], mscratch[par].rearrange("(a h) s -> a h s", a=3))\
                    .then_inc(sem("maxima_loaded"), 16)

            def load_expert(stage, e, src):
                if e >= 2:
                    sp.wait_ge(sem(f"e{stage}_down"), B * (e - 1))
                sp.dma_start(EW[e % 2], src[e]).then_inc(sem(f"e{stage}_weights{e % 2}"), 16)

            def attention(grp):
                load_operands(FRONTS.index((GROUPS[grp][0], 0)))
                for front, back, tl in steps(grp):
                    if front is not None:
                        load_maxima(front)
                        if follows(front) is not None:
                            load_operands(front + 1)

            attention(0)
            sp.wait_ge(sem("x_done"), STAGE_FIRST[("ffn", 0)])
            sp.dma_start(tables[:], d["tables"][:, 4:8, :]).then_inc(sem("tables_loaded"), 16)
            attention(1)
            sp.wait_ge(sem("x_done"), STAGE_FIRST[("ffn", 1)])
            for e in range(NE):
                load_expert(1, e, d["experts1"])
            attention(2)
            sp.wait_ge(sem("x_done"), STAGE_FIRST[("ffn", 2)])
            sp.dma_start(WW, d["wide"]).then_inc(sem("wide_loaded"), 16)
            attention(3)
            sp.wait_ge(sem("x_done"), STAGE_FIRST[("ffn", 3)])
            for e in range(NE3):
                load_expert(3, e, d["experts3"])
            for b in range(B):
                sp.wait_ge(sem("result_ready"), b + 1)
                sp.dma_start(out[b].rearrange("(t p) d -> p t d", p=128), OUT[:, b, :, :]).then_inc(sem("stored"), 16)
            sp.wait_ge(sem("stored"), 16 * B)
            sp.wait_ge(sem("mconst_loaded"), 16)


def _constants():
    eye = np.eye(128, dtype=np.float32)
    r = np.arange(128)
    neg = np.float32(-1e30)
    c = {"ident": eye, "center": eye - np.float32(1 / 128), "mean": np.full((128, 128), 1 / 128, np.float32),
         "eps": np.full((128, 1), 1e-5, np.float32), "zero": np.zeros((128, 1), np.float32),
         "iota": np.tile(np.arange(NE, dtype=np.float32), (128, 1))}
    q, k = r[:, None], r[None, :]
    rep = np.zeros((128, 128), np.float32)
    for j in range(4):
        rep[np.arange(32), 32 * j + np.arange(32)] = 1
    mq3 = np.zeros((128, 2, KP), np.float32)
    for t in range(2):
        mq3[:, t, :] = np.where(np.arange(KP)[None, :] > 128 * t + q, neg, 0)
    mr3 = np.zeros((128, 256), np.float32)
    mr3[0:32] = np.where(128 + np.arange(32)[:, None] > np.arange(256)[None, :], neg, 0)
    dist = np.abs(np.arange(384)[None, :] - 128 - q)
    left = np.where(dist < 10, (dist - 10) * 0.01, 0).astype(np.float32)
    band = np.zeros((128, 3, 384), np.float32)
    for i in range(3):
        band[:, i] = (left.view(np.uint32) & np.uint32(0xFFFF0000)).view(np.float32)
        left = left - band[:, i]
    bf = {"ident": eye, "tri_qk": np.where(k > q, neg, 0), "tri_kq": np.where(q > k, neg, 0), "rep": rep,
          "lower": (q < k).astype(np.float32), "ones": np.ones((128, 128), np.float32),
          "mq3": mq3.reshape(128, 320), "mr3": mr3, "band": band.reshape(128, 1152)}
    const = np.concatenate([np.asarray(bf[n], np.float32) for n, _ in CONST], 1)
    t = np.arange(S, dtype=np.float32)
    e = np.arange(DH)
    f0 = (np.float32(1) / np.float32(10000) ** (np.arange(0, DH, 2, dtype=np.float32) / DH))
    a0 = f0[e // 2][:, None] * t[None, :]
    base = (np.arange(0, DH, 2, dtype=np.float32) + np.float32(0.4 * DH)) / np.float32(1.4 * DH)
    sc = base[e % 4][:, None] ** ((t - S // 2) / np.float32(512.0))[None, :]
    s0 = np.where(e % 2 == 0, -1, 1)[:, None]
    f2 = np.float32(1) / np.float32(10000) ** (np.arange(DH // 2, dtype=np.float32) / (DH // 2))
    a2 = f2[e % 4][:, None] * t[None, :]
    s2 = np.where(e < 4, -1, 1)[:, None]
    q0, q2 = 128 ** -0.5, 8 ** -0.5
    tabs = [np.cos(a0) * sc * q0, s0 * np.sin(a0) * sc * q0, np.cos(a0) / sc, s0 * np.sin(a0) / sc,
            np.cos(a2) * q2, s2 * np.sin(a2) * q2, np.cos(a2), s2 * np.sin(a2)]
    tables = np.stack([np.tile(x.astype(np.float32), (H, 1)) for x in tabs], 1)
    pieces, left = [], np.float32(1e8)
    for i in range(3):
        pieces.append((np.array([left], np.float32).view(np.uint32) & np.uint32(0xFFFF0000)).view(np.float32)[0])
        left = np.float32(left - pieces[-1])
    return c, const, tables, np.array(pieces, np.float32).reshape(3, 1)


def kernel(**inputs):
    import concourse.bacc as bacc
    from concourse.bass_utils import run_bass_kernel_spmd

    a = {k: np.asarray(v) for k, v in inputs.items()}
    c, const, tables, mconst = _constants()
    blocks = dict(c)
    swap = np.arange(D).reshape(-1, 2)[:, ::-1].reshape(-1)
    half = np.arange(D).reshape(H, 2, DH // 2)[:, ::-1].reshape(-1)

    def col(v):
        return v.reshape(-1, 128).T

    def wt(w):
        return w.T

    p = {"wq": a["L0_attn_Wq"], "wk": a["L0_attn_Wv"], "wv": a["L0_attn_Wk"], "wo": a["L0_attn_Wo"]}
    blocks.update({f"L0a.{n}": wt(w) for n, w in p.items()})
    blocks.update({"L0a.wq_rot": wt(p["wq"][swap]), "L0a.wk_rot": wt(p["wk"][swap])})
    bq, bk = a["L0_attn_bq"], a["L0_attn_bv"]
    blocks.update({"L0a.bq": col(bq), "L0a.bq_rot": col(bq[swap]), "L0a.bk": col(bk), "L0a.bk_rot": col(bk[swap]),
                   "L0a.bv": col(a["L0_attn_bk"]), "L0a.bo": col(a["L0_attn_bo"]), "split": np.zeros((128, 0), np.float32)})
    for n, m in (("q", "q"), ("k", "k"), ("v", "v"), ("o", "out")):
        blocks[f"L0x.w{n}"] = wt(a[f"L0_xattn_w_{m}"])
        blocks[f"L0x.b{n}"] = col(a[f"L0_xattn_b_{m}"])
        for l in (1, 3):
            blocks[f"L{l}x.w{n}"] = wt(a[f"L{l}_xattn_W{n}"])
            blocks[f"L{l}x.b{n}"] = col(a[f"L{l}_xattn_b{n}"])
    blocks["f0.w1"] = a["L0_ffn_w1"].T
    blocks["f0.w2"] = a["L0_ffn_w2"].reshape(128, FC, 128).transpose(2, 1, 0).reshape(128, 512)
    blocks["f0.taps"] = a["L0_ffn_conv_w"].reshape(FC, 128, 3).transpose(1, 0, 2).reshape(128, 12)
    blocks["f0.bias"] = col(a["L0_ffn_conv_b"])
    qkv = a["L1_attn_Wqkv"].reshape(H, 3, DH, D)
    blocks["L1a.wqkv"] = qkv.transpose(3, 1, 0, 2).reshape(D, 3 * D)
    blocks["L1a.wo"] = wt(a["L1_attn_Wproj"])
    blocks["L1a.bo"] = col(a["L1_attn_bproj"])
    blocks["f1.router"] = a["L1_ffn_router_w"]
    w2 = a["L2_attn_W_qkv"]
    blocks.update({"L2a.wq": w2[:, 0:D], "L2a.wq_rot": w2[:, 0:D][:, half], "L2a.wk": w2[:, D:2 * D],
                   "L2a.wk_rot": w2[:, D:2 * D][:, half], "L2a.wv": w2[:, 2 * D:], "L2a.wo": a["L2_attn_W_o"]})
    for n in "qkv":
        m = np.zeros((H, DH, H, DH), np.float32)
        m[np.arange(H), :, np.arange(H), :] = a[f"L2_xattn_W{n}"].T
        blocks[f"L2x.w{n}"] = m.reshape(D, D)
    blocks["L2x.wo"] = wt(a["L2_xattn_Wo"])
    blocks["L2x.bo"] = col(a["L2_xattn_bo"])
    for n, m in (("s1", "w1_s"), ("s2", "w2_s"), ("sh1", "h1_s"), ("sh2", "h2_s"), ("s3", "w3_s")):
        blocks[f"f2.{n}"] = col(a[f"L2_ffn_{m}"])
    blocks["L3a.w"] = a["L3_attn_W"]
    blocks["L3a.b"] = col(a["L3_attn_b"])
    blocks["f3.router"] = a["L3_ffn_Wr"]
    blocks["f3.temperature"] = np.broadcast_to(a["L3_ffn_temperature"].reshape(1, 1), (128, 1))
    pack = np.concatenate([blocks[n] for n, _ in PACK], 1)

    def by_rows(w):
        o, i = w.shape
        return w.reshape(o, i // 128, 128).transpose(2, 1, 0).reshape(128, -1)
    wide = np.concatenate([a["L2_ffn_w1_w"].T, a["L2_ffn_w2_w"].T, by_rows(a["L2_ffn_h1_w"]), by_rows(a["L2_ffn_h2_w"]),
                           by_rows(a["L2_ffn_w3_w"])], 1)
    ctx = np.zeros((B, KP, D), np.float32)
    ctx[:, :KC] = a["ctx_1024"]
    mk = np.zeros((S, KP), np.bool_)
    mk[:, :KC] = a["mask_1x1xSxS2_bk0"].reshape(S, KC)
    mc = np.zeros((B, KP), np.bool_)
    mc[:, :KC] = a["mask_BxS2_bf1"]
    arrays = {
        "xT": a["x"].transpose(2, 0, 1), "cT": ctx.transpose(2, 0, 1), "pack": pack, "wide": wide, "const": const,
        "tables": tables, "mconst": mconst,
        "mask_q": mk.reshape(QT, 128, KP).transpose(1, 0, 2).reshape(128, QT * KP), "mask_k": mk.T,
        "mask_c": mc.reshape(1, B * KP),
        "experts1": np.concatenate([a["L1_ffn_gate_w"], a["L1_ffn_up_w"], a["L1_ffn_down_w"]], 2),
        "experts3": np.concatenate([a["L3_ffn_Wg"], a["L3_ffn_Wu"], a["L3_ffn_Wd"]], 2),
        "zrow": np.zeros((3, H, S // 2), np.float32),
    }
    arrays = {k: np.ascontiguousarray(v) for k, v in arrays.items()}
    nc = bacc.Bacc("TRN2", target_bir_lowering=False, num_devices=1)
    d = {k: nc.dram_tensor("in_" + k, v.shape, mybir.dt.from_np(v.dtype), kind="ExternalInput").ap() for k, v in arrays.items()}
    d["zrow"] = d["zrow"].bitcast(BF16)
    out = nc.dram_tensor("out", (B, S, D), F32, kind="ExternalOutput").ap()
    program(nc, d, out)
    r = run_bass_kernel_spmd(nc, [{"in_" + k: v for k, v in arrays.items()}], core_ids=[0])
    return r.results[0]["out"]
```
